# Optimizing a Trainium2 kernel written in Bass

```python
import numpy as np
import jax
import jax.numpy as jnp

def _softmax(x, axis=-1):
    return jax.nn.softmax(x, axis=axis)

def _gelu(x):
    return jax.nn.gelu(x, approximate=True)

def _silu(x):
    return jax.nn.silu(x)

def _sigmoid(x):
    return jax.nn.sigmoid(x)

def _layernorm(x, axis=-1, eps=1e-05):
    m = jnp.mean(x, axis=axis, keepdims=True)
    v = jnp.var(x, axis=axis, keepdims=True)
    return (x - m) / jnp.sqrt(v + eps)

def _scatter_add(tgt, idx, src, axis=0):
    return tgt.at[idx].add(src)

def _segment_sum(src, seg, n):
    return jax.ops.segment_sum(src, seg, n)
kernel_name = 'mk_gnn_resnorm_d2_gnn_r32_0d35b0'

def setup_inputs(seed: int=0):
    np.random.seed(seed)
    _w = jnp.asarray

    def _rec_inputs():
        import jax
        import jax.numpy as jnp
        _gk = jax.random.key(seed)
        x = -0.000202 + 1 * jax.random.normal(jax.random.fold_in(_gk, 1), (3125, 128), jnp.float32)
        src = jax.random.randint(jax.random.fold_in(_gk, 2), (100000,), 0, 3125, jnp.int32)
        dst = jnp.minimum((3125 * jax.random.uniform(jax.random.fold_in(_gk, 3), (100000,)) ** 2.0).astype(jnp.int32), 99999)
        _o = jnp.argsort(dst, stable=True)
        src = src[_o]
        dst = dst[_o]
        edge_type_4 = jax.random.randint(jax.random.fold_in(_gk, 13), (100000,), 0, 4, jnp.int32)
        return (x, src, dst, edge_type_4)
    x, src, dst, edge_type_4 = _rec_inputs()

    def _L0_gnn_setup():
        import jax, jax.numpy as jnp
        import numpy as np
        N = 50000
        E = 25000
        D = 128
        H = 8
        DK = D // H
        key = jax.random.key(seed)
        ks = jax.random.split(key, 12)
        s = 1.0 / np.sqrt(D)
        return {'h': jax.random.normal(ks[0], (N, D), dtype=jnp.float32), 'Wq': jax.random.normal(ks[1], (D, D), dtype=jnp.float32) * s, 'bq': jnp.zeros((D,), dtype=jnp.float32), 'Wk': jax.random.normal(ks[2], (D, D), dtype=jnp.float32) * s, 'bk': jnp.zeros((D,), dtype=jnp.float32), 'Wv': jax.random.normal(ks[3], (D, D), dtype=jnp.float32) * s, 'bv': jnp.zeros((D,), dtype=jnp.float32), 'Wo': jax.random.normal(ks[4], (D, D), dtype=jnp.float32) * s, 'bo': jnp.zeros((D,), dtype=jnp.float32), 'src': jax.random.randint(ks[5], (E,), 0, N, dtype=jnp.int64) if jax.config.jax_enable_x64 else jax.random.randint(ks[5], (E,), 0, N, dtype=jnp.int32), 'dst': jax.random.randint(ks[6], (E,), 0, N, dtype=jnp.int32)}
    _L0_gnn_all = _L0_gnn_setup()
    _L0_gnn_in = {k: v for k, v in _L0_gnn_all.items() if k in ('Wq', 'bq', 'Wk', 'bk', 'Wv', 'bv', 'Wo', 'bo')}
    del _L0_gnn_all

    def _L1_gnn_setup():
        import jax, jax.numpy as jnp
        import numpy as np
        N_NODES = 50000
        N_EDGES = 18750
        DIM = 128
        N_EDGE_TYPES = 4
        N_STEPS = 4

        def _gru_cell(x, h, w_ih, w_hh, b_ih, b_hh):
            gi = x @ w_ih.T + b_ih
            gh = h @ w_hh.T + b_hh
            i_r, i_z, i_n = jnp.split(gi, 3, axis=-1)
            h_r, h_z, h_n = jnp.split(gh, 3, axis=-1)
            r = jax.nn.sigmoid(i_r + h_r)
            z = jax.nn.sigmoid(i_z + h_z)
            n = jnp.tanh(i_n + r * h_n)
            return (1.0 - z) * n + z * h

        def _step(embedding, src, dst, etype, W_msg, b_msg, w_ih, w_hh, b_ih, b_hh):
            n = embedding.shape[0]
            m = (embedding @ W_msg.T + b_msg).reshape(n, N_EDGE_TYPES, DIM)
            q = m[src, etype]
            r = jax.ops.segment_sum(q, dst, num_segments=n)
            return _gru_cell(r, embedding, w_ih, w_hh, b_ih, b_hh)
        key = jax.random.key(seed)
        ks = jax.random.split(key, 9)
        bound = 1.0 / np.sqrt(DIM)
        return {'embedding': jax.random.normal(ks[0], (N_NODES, DIM), dtype=jnp.float32), 'edge_uv': jax.random.randint(ks[1], (2, N_EDGES), 0, N_NODES, dtype=jnp.int64), 'edge_type': jax.random.randint(ks[2], (N_EDGES,), 0, N_EDGE_TYPES, dtype=jnp.int64), 'W_msg': jax.random.uniform(ks[3], (DIM * N_EDGE_TYPES, DIM), jnp.float32, -bound, bound), 'b_msg': jax.random.uniform(ks[4], (DIM * N_EDGE_TYPES,), jnp.float32, -bound, bound), 'w_ih': jax.random.uniform(ks[5], (3 * DIM, DIM), jnp.float32, -bound, bound), 'w_hh': jax.random.uniform(ks[6], (3 * DIM, DIM), jnp.float32, -bound, bound), 'b_ih': jax.random.uniform(ks[7], (3 * DIM,), jnp.float32, -bound, bound), 'b_hh': jax.random.uniform(ks[8], (3 * DIM,), jnp.float32, -bound, bound)}
    _L1_gnn_all = _L1_gnn_setup()
    _L1_gnn_in = {k: v for k, v in _L1_gnn_all.items() if k in ('W_msg', 'b_msg', 'w_ih', 'w_hh', 'b_ih', 'b_hh')}
    del _L1_gnn_all
    return {'x': x, 'src': src, 'dst': dst, 'edge_type_4': edge_type_4, 'L0_gnn_Wq': _L0_gnn_in['Wq'], 'L0_gnn_bq': _L0_gnn_in['bq'], 'L0_gnn_Wk': _L0_gnn_in['Wk'], 'L0_gnn_bk': _L0_gnn_in['bk'], 'L0_gnn_Wv': _L0_gnn_in['Wv'], 'L0_gnn_bv': _L0_gnn_in['bv'], 'L0_gnn_Wo': _L0_gnn_in['Wo'], 'L0_gnn_bo': _L0_gnn_in['bo'], 'L1_gnn_W_msg': _L1_gnn_in['W_msg'], 'L1_gnn_b_msg': _L1_gnn_in['b_msg'], 'L1_gnn_w_ih': _L1_gnn_in['w_ih'], 'L1_gnn_w_hh': _L1_gnn_in['w_hh'], 'L1_gnn_b_ih': _L1_gnn_in['b_ih'], 'L1_gnn_b_hh': _L1_gnn_in['b_hh']}

def reference(x, src, dst, edge_type_4, L0_gnn_Wq, L0_gnn_bq, L0_gnn_Wk, L0_gnn_bk, L0_gnn_Wv, L0_gnn_bv, L0_gnn_Wo, L0_gnn_bo, L1_gnn_W_msg, L1_gnn_b_msg, L1_gnn_w_ih, L1_gnn_w_hh, L1_gnn_b_ih, L1_gnn_b_hh):
    import jax
    import jax.numpy as jnp

    def _L0_gnn_ref(h, Wq, bq, Wk, bk, Wv, bv, Wo, bo, src, dst):
        import jax, jax.numpy as jnp
        import numpy as np
        N = 50000
        E = 25000
        D = 128
        H = 8
        DK = D // H
        n = h.shape[0]
        scale = jnp.asarray(np.sqrt(DK), dtype=h.dtype)
        q = (h @ Wq.T + bq).reshape(n, H, DK)
        k = (h @ Wk.T + bk).reshape(n, H, DK)
        v = (h @ Wv.T + bv).reshape(n, H, DK)
        score = jnp.einsum('ehd,ehd->eh', q[dst], k[src]) / scale
        m = jax.ops.segment_max(score, dst, num_segments=n)
        ex = jnp.exp(score - m[dst])
        denom = jax.ops.segment_sum(ex, dst, num_segments=n)
        alpha = ex / denom[dst]
        msg = v[src] * alpha[:, :, None]
        att = jax.ops.segment_sum(msg, dst, num_segments=n).reshape(n, D)
        return att @ Wo.T + bo

    def _L1_gnn_ref(embedding, edge_uv, edge_type, W_msg, b_msg, w_ih, w_hh, b_ih, b_hh):
        import jax, jax.numpy as jnp
        import numpy as np
        N_NODES = 50000
        N_EDGES = 18750
        DIM = 128
        N_EDGE_TYPES = 4
        N_STEPS = 4

        def _gru_cell(x, h, w_ih, w_hh, b_ih, b_hh):
            gi = x @ w_ih.T + b_ih
            gh = h @ w_hh.T + b_hh
            i_r, i_z, i_n = jnp.split(gi, 3, axis=-1)
            h_r, h_z, h_n = jnp.split(gh, 3, axis=-1)
            r = jax.nn.sigmoid(i_r + h_r)
            z = jax.nn.sigmoid(i_z + h_z)
            n = jnp.tanh(i_n + r * h_n)
            return (1.0 - z) * n + z * h

        def _step(embedding, src, dst, etype, W_msg, b_msg, w_ih, w_hh, b_ih, b_hh):
            n = embedding.shape[0]
            m = (embedding @ W_msg.T + b_msg).reshape(n, N_EDGE_TYPES, DIM)
            q = m[src, etype]
            r = jax.ops.segment_sum(q, dst, num_segments=n)
            return _gru_cell(r, embedding, w_ih, w_hh, b_ih, b_hh)
        src, dst = (edge_uv[0], edge_uv[1])
        for _ in range(N_STEPS):
            embedding = _step(embedding, src, dst, edge_type, W_msg, b_msg, w_ih, w_hh, b_ih, b_hh)
        return embedding
    edge_index = jnp.stack([src, dst])
    x = _layernorm(x + _L0_gnn_ref(x, L0_gnn_Wq, L0_gnn_bq, L0_gnn_Wk, L0_gnn_bk, L0_gnn_Wv, L0_gnn_bv, L0_gnn_Wo, L0_gnn_bo, src, dst), axis=-1)
    x = _layernorm(x + _L1_gnn_ref(x, edge_index, edge_type_4, L1_gnn_W_msg, L1_gnn_b_msg, L1_gnn_w_ih, L1_gnn_w_hh, L1_gnn_b_ih, L1_gnn_b_hh), axis=-1)
    return x

_drawn_inputs = setup_inputs


def setup_inputs(seed=0):
    import zlib

    import numpy as np

    out = dict(_drawn_inputs(seed))
    spreads = {'L0_gnn_bq': (0.0, 0.1),
     'L0_gnn_bk': (0.0, 0.1),
     'L0_gnn_bv': (0.0, 0.1),
     'L0_gnn_bo': (0.0, 0.1)}
    factors = {}
    for name, (base, spread) in spreads.items():
        noise = np.random.default_rng([zlib.crc32(name.encode()), seed]).standard_normal(out[name].shape)
        drawn = base * np.exp(spread * noise) if base else spread * noise
        out[name] = jnp.asarray(drawn.astype(out[name].dtype))
    for name, factor in factors.items():
        out[name] = (out[name] * factor).astype(out[name].dtype)
    return out
```

```python
import concourse.bass as bass
from concourse import mybir
from contextlib import ExitStack


def gnn_program(nc, x, src, dst, etype, Wq, bq, Wk, bk, Wv, bv, Wo, bo, W_msg, b_msg,
                w_ih, w_hh, b_ih, b_hh, out):
    f32, bf16, i32 = mybir.dt.float32, mybir.dt.bfloat16, mybir.dt.int32
    ALU = mybir.AluOpType
    ACT = mybir.ActivationFunctionType
    AX = mybir.AxisListType.X

    P = 128
    NODES, D = x.shape
    EDGES = src.shape[0]
    HEADS = 8
    DK = D // HEADS
    TYPES = W_msg.shape[0] // D
    STEPS = 4
    EPS = 1e-5
    BIG = 1.0e30
    BLOCKS = (NODES + P - 1) // P
    PADN = BLOCKS * P
    TAILN = NODES - (BLOCKS - 1) * P
    FULLT = EDGES // P
    TAILE = EDGES - FULLT * P
    TILES = FULLT + (TAILE > 0)
    GRP, GROUPS = 4, 4
    TURN = GRP * GROUPS
    TURNS = (TILES + BLOCKS - 1 + TURN - 1) // TURN
    VISITS = TURNS * TURN
    VROWS = (VISITS + P - 1) // P
    VPAD = VROWS * P
    NO_NODE = 1 << 20
    CHUNKS = P // HEADS
    VPC = VISITS // CHUNKS
    SEQ = VPC * P
    assert CHUNKS * VPC == VISITS
    BANK = 512
    ACC_BANKS = (PADN + BANK - 1) // BANK
    CH = [(c * BANK, min(BANK, PADN - c * BANK)) for c in range(ACC_BANKS)]

    ctx = ExitStack()
    with ctx:
        def sb(name, shape, dt):
            return ctx.enter_context(nc.sbuf_tensor(name, shape, dt))

        def sem(name):
            return ctx.enter_context(nc.semaphore(name))

        class Chain:

            def __init__(self, eng, name):
                self.eng, self.sem, self.base, self.n = eng, sem(name), 0, 0

            def turn(self, turn, per_turn):
                self.base, self.n = turn * per_turn, 0

            def link(self, instruction):
                self.n += 1
                instruction.then_inc(self.sem, 1)
                self.eng.wait_ge(self.sem, self.base + self.n)

        kv_d = nc.dram_tensor("kv_rows", [PADN, 2 * D], f32, kind="Internal").ap()
        msg_d = nc.dram_tensor("msg_rows", [PADN * TYPES, D], f32, kind="Internal").ap()
        v_d = nc.dram_tensor("v_of_visits", [P, VISITS, D], f32, kind="Internal").ap()
        edges_d = nc.dram_tensor("edge_tiles", [VPAD, 3 * P], i32, kind="Internal").ap()
        edges_v = edges_d.rearrange("t (k e) -> t k e", k=3)

        PS = ctx.enter_context(nc.psum_tensor("PS", [P, 8 * BANK], f32))

        def bank(k, n=BANK):
            return PS[:, k * BANK:k * BANK + n]

        ident = sb("ident", [P, P], f32)
        identb = sb("identb", [P, P], bf16)
        iota_row = sb("iota_row", [P, P], f32)
        iota_col = sb("iota_col", [P, 1], f32)
        iota_visit = sb("iota_visit", [P, VPAD], f32)
        visit_col = sb("visit_col", [P, VROWS], f32)
        visit_i = sb("visit_i", [P, VROWS], i32)
        ints = sb("ints", [P, VPAD], i32)
        ones = sb("ones", [P, P], f32)
        zerob = sb("zerob", [P, BANK], bf16)
        pad_rows = sb("pad_rows", [P, 3 * P], i32)
        last_dst = sb("last_dst", [P, VROWS], i32)
        last_dstf = sb("last_dstf", [P, VROWS], f32)
        limit = sb("limit", [P, BLOCKS - 1], f32)
        below = sb("below", [P, VROWS, BLOCKS - 1], f32)
        leave = sb("leave", [BLOCKS - 1, 1], f32)
        passed = sb("passed", [BLOCKS - 1, VPAD], f32)
        block_first = sb("block_first", [P, VROWS], f32)
        tile_f = sb("tile_f", [P, VROWS], f32)
        tile_i = sb("tile_i", [P, VROWS], i32)
        visit_off = sb("visit_off", [1, VPAD], i32)
        rel = sb("rel", [P, VPAD], f32)
        key = sb("key", [P, VPC + VPAD + VPC], f32)
        src_i = sb("src_i", [P, VPAD], i32)
        pair_i = sb("pair_i", [P, VPAD], i32)
        stage = sb("stage", [P, GROUPS, GRP], i32)
        scores = sb("scores", [P, VISITS, HEADS], f32)
        wqkvT = sb("wqkvT", [P, 3 * D], f32)
        woT = sb("woT", [P, D], f32)
        wmsgT = sb("wmsgT", [P, TYPES * D], f32)
        wihT = sb("wihT", [P, 3 * D], f32)
        whhT = sb("whhT", [P, 3 * D], f32)
        bqkv_b = sb("bqkv_b", [P, 3 * D], f32)
        bo_b = sb("bo_b", [P, D], f32)
        bmsg_b = sb("bmsg_b", [P, TYPES * D], f32)
        bih = sb("bih", [P, 3], f32)
        bhh = sb("bhh", [P, 3], f32)
        brz = sb("brz", [P, 2], f32)
        col_last = sb("col_last", [P, 1], f32)
        col_pass = sb("col_pass", [P, 1], f32)
        col_carry = sb("col_carry", [P, 1], f32)
        row_last = sb("row_last", [1, P], f32)
        row_pass = sb("row_pass", [1, P], f32)
        row_end = sb("row_end", [1, P], f32)
        row_carry = sb("row_carry", [1, P], f32)
        ln_sum = sb("ln_sum", [P, BLOCKS], f32)
        ln_var = sb("ln_var", [P, BLOCKS], f32)
        eps_col = sb("eps_col", [P, 1], f32)

        region = sb("region", [P, 4 * (SEQ + 2 * P)], f32)
        cut_at = [0]

        def cut(n):
            cut_at[0] += n
            assert cut_at[0] <= 4 * (SEQ + 2 * P)
            return region[:, cut_at[0] - n:cut_at[0]]

        x_nat = cut(PADN)
        xT = cut(PADN)
        q_nat = cut(PADN)
        base_tables = cut_at[0]
        kv_st = cut(2 * PADN)
        visit_edges = cut(VROWS * 3 * P).bitcast(i32).rearrange("p (r k e) -> p r k e", r=VROWS, k=3)
        dst_v, rel_v, ge0_v, key_v, src_v, pair_v = (
            cut(VPAD).rearrange("p (r e) -> p r e", r=VROWS) for _ in range(6))
        cut_at[0] = base_tables
        kv_g = cut(TURN * 2 * D).rearrange("p (g j c) -> p g j c", g=GROUPS, j=GRP)
        onehot_b = cut(GROUPS * GRP * P // 2).bitcast(bf16).rearrange("p (g j e) -> p g j e", g=GROUPS, j=GRP)
        onehotT = cut(GROUPS * GRP * P).rearrange("p (g j e) -> p g j e", g=GROUPS, j=GRP)
        prod = cut(2 * GRP * D).rearrange("p (g c) -> p g c", g=2)
        w_nat = region[:, 4 * (SEQ + 2 * P) - 14 * P:4 * (SEQ + 2 * P)].rearrange("p (k c) -> p k c", k=14)
        cut_at[0] = 0
        seq_s, seq_r, seq_a, seq_b = (cut(SEQ + 2 * P) for _ in range(4))
        cut_at[0] = 0
        x_again = cut(PADN)
        x1 = cut(PADN)
        hT = cut(PADN)
        sumT = cut(PADN)
        g_ring = cut(TURN * D).rearrange("p (g j c) -> p g j c", g=GROUPS, j=GRP)
        onehot = cut(GROUPS * GRP * P).rearrange("p (g j e) -> p g j e", g=GROUPS, j=GRP)
        av = cut(TURN * D).rearrange("p (g j c) -> p g j c", g=GROUPS, j=GRP)
        msg_st = cut(4 * TYPES * D).rearrange("p (s c) -> p s c", s=4)
        gates = cut(2 * 3 * BANK).rearrange("p (s k n) -> p s k n", s=2, k=3)

        s_w, s_x, s_b, s_pad, s_iota = sem("weights_in"), sem("x_in"), sem("bias_in"), sem("pad_rows_set"), sem("iota_done")
        s_edges, s_last = sem("edge_tiles_written"), sem("last_dst_in")
        s_const, s_xpad = sem("constants_set"), sem("x_padding_zeroed")
        s_wt, s_wc = sem("weights_transposed"), sem("weights_copied")
        s_xt, s_xc = sem("x_transposed"), sem("xT_copied")
        s_qkv, s_qkvc, s_kvd = sem("qkv_ready"), sem("qkv_copied"), sem("kv_rows_written")
        s_below, s_left, s_passed, s_blk = sem("below_ready"), sem("tiles_before_ready"), sem("passed_ready"), sem("visit_blocks_ready")
        s_tile, s_ve, s_vf, s_vt = sem("visit_tiles_ready"), sem("visit_edges_in"), sem("visit_fields_ready"), sem("fields_transposed")
        s_vfree, s_vi, s_off = sem("field_bank_free"), sem("visit_arrays_ready"), sem("visit_offsets_ready")
        s_g = [sem(f"kv_gathered{g}") for g in range(GROUPS)]
        s_stage, s_gfree = sem("indices_staged"), sem("kv_group_scored")
        s_vsp = [sem(f"v_spilled{g}") for g in range(GROUPS)]
        s_oh, s_oht, s_ohtc, s_qe, s_pr = sem("onehot_built"), sem("onehot_transposed"), sem("onehotT_copied"), sem("q_of_edges_ready"), sem("q_bank_read")
        s_keyx, s_scx = sem("keys_spread"), sem("scores_spread")
        s_keyT, s_keyTc, s_scT, s_scTc = sem("key_transposed"), sem("keyT_copied"), sem("score_transposed"), sem("scoreT_copied")
        s_cr, s_crc, s_cc = sem("carry_rows_ready"), sem("carry_row_set"), sem("carry_column_ready")
        s_cols, s_sub, s_exp = sem("carry_inputs_set"), sem("score_less_max"), sem("exp_done")
        s_alpha, s_alT, s_alc = sem("alpha_ready"), sem("alpha_transposed"), sem("alpha_copied")
        s_vin = [sem(f"v_loaded{g}") for g in range(GROUPS)]
        s_av, s_sum = sem("weighted_v_ready"), sem("att_group_summed")
        s_zero = sem("sum_banks_zeroed")
        s_attc, s_o, s_x2, s_res = sem("att_copied"), sem("o_product_ready"), sem("x_again_in"), sem("residual_ready")
        s_lnv, s_lnr, s_lnc, s_sq = sem("ln_centred"), sem("ln_root"), sem("ln_varsum"), sem("ln_squared")
        s_x1, s_ht, s_htc = sem("x1_ready"), sem("x1_transposed"), sem("hT_copied")
        s_m, s_mc = sem("messages_ready"), sem("messages_copied")
        s_md = [sem(f"msg_rows_written{k}") for k in range(4)]
        s_mg = [sem(f"msg_gathered{g}") for g in range(GROUPS)]
        s_mstage, s_moh, s_msum = sem("msg_indices_staged"), sem("msg_onehot_built"), sem("msg_group_summed")
        s_sumA, s_sumV = sem("sum_copied_act"), sem("sum_copied_dve")
        s_gate, s_rz, s_npre, s_tanh, s_h = sem("gates_ready"), sem("rz_ready"), sem("n_input_ready"), sem("tanh_ready"), sem("h_updated")
        s_fin, s_y, s_out = sem("h_transposed"), sem("y_ready"), sem("out_written")

        block = ctx.enter_context(nc.Block())
        weights = ([Wq, Wk, Wv, Wo] + [W_msg[k * D:(k + 1) * D, :] for k in range(TYPES)]
                   + [w_ih[k * D:(k + 1) * D, :] for k in range(3)] + [w_hh[k * D:(k + 1) * D, :] for k in range(3)])
        NW = len(weights)
        wT = ([wqkvT[:, k * D:(k + 1) * D] for k in range(3)] + [woT[:, :]]
              + [wmsgT[:, k * D:(k + 1) * D] for k in range(TYPES)]
              + [wihT[:, k * D:(k + 1) * D] for k in range(3)] + [whhT[:, k * D:(k + 1) * D] for k in range(3)])
        W_BATCHES = [(k, min(4, NW - k)) for k in range(0, NW, 4)]
        X_BATCHES = [(k, min(4, BLOCKS - k)) for k in range(0, BLOCKS, 4)]
        G_BATCHES = [(k, min(4, VPC - k)) for k in range(0, VPC, 4)]
        FIELD_PARTS = [(0, 4), (4, VROWS - 4)]
        biases = ([(bqkv_b[:, k * D:(k + 1) * D], b) for k, b in enumerate((bq, bk, bv))]
                  + [(bo_b[:, :], bo), (bmsg_b[:, :], b_msg)])

        @block.sync
        def _(sp):
            sp.wait_ge(s_pad, 2)
            for k, a in enumerate((src, dst, etype)):
                sp.dma_start(edges_v[0:FULLT, k, :], a[0:FULLT * P].rearrange("(t e) -> t e", e=P)).then_inc(s_edges, 16)
                sp.dma_start(edges_v[FULLT:TILES, k, 0:TAILE], a[FULLT * P:EDGES].rearrange("(t e) -> t e", t=1)).then_inc(s_edges, 16)
                sp.dma_start(edges_v[FULLT:TILES, k, TAILE:P], pad_rows[0:1, k * P + TAILE:(k + 1) * P]).then_inc(s_edges, 16)
            sp.dma_start(edges_d[TILES:VPAD, :], pad_rows[0:VPAD - TILES, :]).then_inc(s_edges, 16)
            for k, w in enumerate(weights):
                sp.dma_start(w_nat[:, k, :], w).then_inc(s_w, 16)
            sp.wait_ge(s_xpad, 1)
            full = (BLOCKS - 1) * P
            sp.dma_start(x_nat[:, 0:full].rearrange("p (b c) -> p b c", c=D),
                         x[0:full, :].rearrange("(b p) c -> p b c", p=P)).then_inc(s_x, 16)
            sp.dma_start(x_nat[0:TAILN, full:full + D], x[full:NODES, :]).then_inc(s_x, 16)
            for to, b in biases:
                sp.dma_start(to, b.rearrange("(a n) -> a n", a=1).broadcast_to([P, b.shape[0]])).then_inc(s_b, 16)
            for to, b in ((bih, b_ih), (bhh, b_hh)):
                with nc.allow_non_contiguous_dma(reason="a few hundred bias elements"):
                    sp.dma_start(to[:, :], b.rearrange("(k p) -> p k", p=P)).then_inc(s_b, 16)
            sp.wait_ge(s_edges, 16 * 10)
            with nc.allow_non_contiguous_dma(reason="one element of each tile"):
                sp.dma_start(last_dst[:, :], edges_d.rearrange("(r p) c -> p r c", p=P)[:, :, 2 * P - 1:2 * P].rearrange("p r c -> p (r c)")).then_inc(s_last, 16)
            for n, (b0, nb) in enumerate(X_BATCHES):
                sp.wait_ge(s_qkvc, b0 + nb)
                sp.dma_start(kv_d[b0 * P:(b0 + nb) * P, :].rearrange("(b p) c -> p b c", p=P),
                             kv_st[:, b0 * 2 * D:(b0 + nb) * 2 * D].rearrange("p (b c) -> p b c", b=nb)).then_inc(s_kvd, 16)
            for g in range(GROUPS):
                sp.sem_inc(s_vsp[g], 16)
            with sp.Fori(0, TURNS) as i:
                for g in range(GROUPS):
                    sp.wait_ge(s_g[g], 16 * GRP * (i + 1))
                    sp.dma_start(v_d[:, bass.ds(i * TURN + g * GRP, GRP), :], kv_g[:, g, :, D:2 * D]).then_inc(s_vsp[g], 16)
            sp.wait_ge(s_alT, len(G_BATCHES))
            sp.wait_ge(s_xpad, 2)
            sp.dma_start(x_again[:, 0:full].rearrange("p (b c) -> p b c", c=D),
                         x[0:full, :].rearrange("(b p) c -> p b c", p=P)).then_inc(s_x2, 16)
            sp.dma_start(x_again[0:TAILN, full:full + D], x[full:NODES, :]).then_inc(s_x2, 16)
            for g in range(GROUPS):
                sp.wait_ge(s_vsp[g], 16 * (TURNS + 1))
            with sp.Fori(0, TURNS) as i:
                for g in range(GROUPS):
                    sp.wait_ge(s_av, i * GROUPS + g + 1)
                    sp.dma_start(g_ring[:, g, :, :], v_d[:, bass.ds(i * TURN + g * GRP, GRP), :]).then_inc(s_vin[g], 16)
            with sp.Fori(0, STEPS) as s:
                for b in range(BLOCKS):
                    sp.wait_ge(s_mc, s * BLOCKS + b + 1)
                    sp.dma_start(msg_d[b * P * TYPES:(b + 1) * P * TYPES, :].rearrange("(p t) c -> p (t c)", p=P),
                                 msg_st[:, b % 4, :]).then_inc(s_md[b % 4], 16)
            sp.wait_ge(s_y, 1)
            sp.dma_start(out[0:full, :].rearrange("(b p) c -> p b c", p=P),
                         x_again[:, 0:full].rearrange("p (b c) -> p b c", c=D)).then_inc(s_out, 16)
            sp.dma_start(out[full:NODES, :], x_again[0:TAILN, full:full + D]).then_inc(s_out, 16)
            sp.wait_ge(s_out, 32)

        @block.gpsimd
        def _(pool):
            ch = Chain(pool, "pool_chain")
            ch.link(nc.gpsimd.memset(pad_rows[:, :], 0))
            nc.gpsimd.memset(pad_rows[:, P:2 * P], NO_NODE).then_inc(s_pad, 2)
            nc.gpsimd.iota(ints[:, :], [[1, VPAD]], base=0, channel_multiplier=0).then_inc(s_iota, 1)
            nc.gpsimd.iota(visit_i[:, :], [[P, VROWS]], base=0, channel_multiplier=1).then_inc(s_iota, 1)
            pool.wait_ge(s_edges, 16 * 10)
            pool.wait_ge(s_tile, 1)
            for r in range(VROWS):
                nc.gpsimd.indirect_dma_start(
                    out=visit_edges[:, r, :, :].rearrange("p k e -> p (k e)"), out_offset=None, in_=edges_d[:, :],
                    in_offset=bass.IndirectOffsetOnAxis(ap=tile_i[:, r:r + 1], axis=0)).then_inc(s_ve, 16)
            pool.wait_ge(s_kvd, 16 * len(X_BATCHES))
            pool.wait_ge(s_vt, 2)
            with pool.Fori(0, TURNS) as i:
                for g in range(GROUPS):
                    pool.wait_ge(s_gfree, i * GROUPS + g + 1)
                    pool.wait_ge(s_vsp[g], 16 * (i + 1))
                    pool.wait_ge(s_stage, i * GROUPS + g + 1)
                    pool.nop(nofuse=True)
                    for j in range(GRP):
                        nc.gpsimd.indirect_dma_start(
                            out=kv_g[:, g, j, :], out_offset=None, in_=kv_d[:, :],
                            in_offset=bass.IndirectOffsetOnAxis(ap=stage[:, g, j:j + 1], axis=0)).then_inc(s_g[g], 16)
            with pool.Fori(0, STEPS) as s:
                for k in range(4):
                    pool.wait_ge(s_md[k], 16 * len(range(k, BLOCKS, 4)) * (s + 1) + 16)
                pool.nop(nofuse=True)
                with pool.Fori(0, TURNS) as i:
                    for g in range(GROUPS):
                        pool.wait_ge(s_msum, (s * TURNS + i) * GROUPS + g + 1)
                        pool.wait_ge(s_mstage, (s * TURNS + i) * GROUPS + g + 1)
                        pool.nop(nofuse=True)
                        for j in range(GRP):
                            nc.gpsimd.indirect_dma_start(
                                out=g_ring[:, g, j, :], out_offset=None, in_=msg_d[:, :],
                                in_offset=bass.IndirectOffsetOnAxis(ap=stage[:, g, j:j + 1], axis=0)).then_inc(s_mg[g], 16)

        @block.scalar
        def _(act):
            ch = Chain(act, "act_chain")
            for n, (k0, nk) in enumerate(W_BATCHES):
                act.wait_ge(s_wt, n + 1)
                for k in range(k0, k0 + nk):
                    last = nc.scalar.copy(wT[k], bank(n % 2)[:, (k - k0) * D:(k - k0 + 1) * D])
                last.then_inc(s_wc, 1)
            for n, (b0, nb) in enumerate(X_BATCHES):
                act.wait_ge(s_xt, n + 1)
                nc.scalar.copy(xT[:, b0 * P:(b0 + nb) * P], bank(2 + n % 2)[:, 0:nb * P]).then_inc(s_xc, 1)

            act.wait_ge(s_vi, 1)
            act.wait_ge(s_kvd, 16 * len(X_BATCHES))
            for g in range(GROUPS):
                nc.scalar.copy(stage[:, g, :], src_i[:, g * GRP:(g + 1) * GRP]).then_inc(s_stage, 1)
            with act.Fori(0, TURNS) as i:
                for g in range(GROUPS):
                    act.wait_ge(s_oht, i * GROUPS + g + 1)
                    nc.scalar.copy(onehotT[:, g, :, :], bank(g % 2).bitcast(bf16)[:, 0:GRP * P].rearrange("p (j e) -> p j e", j=GRP)).then_inc(s_ohtc, 1)
                    act.wait_ge(s_g[g], 16 * GRP * (i + 1))
                    act.nop(nofuse=True)
                    nc.scalar.copy(stage[:, g, :], src_i[:, bass.ds(i * TURN + TURN + g * GRP, GRP)]).then_inc(s_stage, 1)

            act.wait_ge(s_gfree, GROUPS * (TURNS + 1))
            for g in range(GROUPS):
                act.wait_ge(s_vsp[g], 16 * (TURNS + 1))
            for g0, ng in ((0, VPC), (VPC, 2)):
                for c in range(CHUNKS):
                    last = nc.scalar.copy(seq_r[:, g0 * P:(g0 + ng) * P].rearrange("p (g c h) -> p g c h", c=CHUNKS, h=HEADS)[:, :, c, :],
                                          key[:, VPC - 1 + g0 + c * VPC:VPC - 1 + g0 + ng + c * VPC].unsqueeze(2).to_broadcast([P, ng, HEADS]))
            last.then_inc(s_keyx, 1)

            act.wait_ge(s_sub, 1)
            nc.scalar.activation(seq_s[:, 0:SEQ], seq_s[:, 0:SEQ], ACT.Exp, scale=float(DK) ** -0.5).then_inc(s_exp, 1)
            al = scores[:, :, :].rearrange("p (c g) h -> p g c h", g=VPC)
            for n, (g0, ng) in enumerate(G_BATCHES):
                act.wait_ge(s_alT, n + 1)
                for g in range(g0, g0 + ng):
                    last = nc.scalar.copy(al[:, g, :, :], bank(n % 2)[:, (g - g0) * P:(g - g0 + 1) * P].rearrange("p (c h) -> p c h", h=HEADS))
                last.then_inc(s_alc, 1)
            act.wait_ge(s_sum, GROUPS * (TURNS + 1))
            for k, (a, n) in enumerate(CH):
                nc.scalar.copy(sumT[:, a:a + n], bank(k, n)).then_inc(s_attc, 1)
            def layernorm_root(turn):
                act.wait_ge(s_lnv, turn)
                nc.scalar.activation(hT[:, :], x1[:, :] if turn == 1 else x_again[:, :], ACT.Square).then_inc(s_sq, 1)
                act.wait_ge(s_lnc, turn)
                nc.scalar.activation(ln_var[:, :], ln_sum[:, :], ACT.Sqrt, bias=eps_col[:, :], scale=1.0 / D).then_inc(s_lnr, 1)
            layernorm_root(1)
            for n, (b0, nb) in enumerate(X_BATCHES):
                act.wait_ge(s_ht, n + 1)
                nc.scalar.copy(hT[:, b0 * P:(b0 + nb) * P], bank(n % 2)[:, 0:nb * P]).then_inc(s_htc, 1)
            for g in range(GROUPS):
                nc.scalar.copy(stage[:, g, :], pair_i[:, g * GRP:(g + 1) * GRP]).then_inc(s_mstage, 1)
            with act.Fori(0, STEPS) as s:
                with act.Fori(0, TURNS) as i:
                    for g in range(GROUPS):
                        act.wait_ge(s_mg[g], 16 * GRP * (s * TURNS + i + 1))
                        act.nop(nofuse=True)
                        nc.scalar.copy(stage[:, g, :], pair_i[:, bass.ds(i * TURN + TURN + g * GRP, GRP)]).then_inc(s_mstage, 1)
                act.wait_ge(s_msum, GROUPS * TURNS * (s + 1) + GROUPS)
                for k in (0, 2, 4, 6):
                    a, n = CH[k]
                    nc.scalar.copy(sumT[:, a:a + n], bank(k, n)).then_inc(s_sumA, 1)
                for k, (a, n) in enumerate(CH):
                    p = k % 2
                    act.wait_ge(s_gate, s * len(CH) + k + 1)
                    nc.scalar.activation(gates[:, p, 0, 0:n], bank(4 * p, n), ACT.Sigmoid, bias=brz[:, 0:1])
                    nc.scalar.activation(gates[:, p, 1, 0:n], bank(4 * p + 1, n), ACT.Sigmoid, bias=brz[:, 1:2]).then_inc(s_rz, 1)
                    act.wait_ge(s_npre, s * len(CH) + k + 1)
                    nc.scalar.activation(gates[:, p, 2, 0:n], gates[:, p, 2, 0:n], ACT.Tanh, bias=bih[:, 2:3]).then_inc(s_tanh, 1)
            layernorm_root(2)

        @block.vector
        def _(dve):
            ch = Chain(dve, "dve_chain")
            link = ch.link
            V = nc.vector
            full = (BLOCKS - 1) * P
            V.memset(x_nat[:, full:full + D], 0.0).then_inc(s_xpad, 1)
            V.memset(zerob[:, :], 0.0)
            V.memset(ones[:, :], 1.0)
            V.memset(eps_col[:, :], EPS)
            V.memset(row_carry[:, :], 0.0)
            V.memset(key[:, 0:VPC], -2.0)
            V.memset(key[:, VPC + VISITS:], -3.0)
            dve.wait_ge(s_iota, 2)
            V.tensor_copy(iota_visit[:, :], ints[:, :])
            V.tensor_copy(iota_row[:, :], ints[:, 0:P])
            link(V.tensor_copy(visit_col[:, :], visit_i[:, :]))
            link(V.tensor_copy(iota_col[:, :], visit_col[:, 0:1]))
            link(V.tensor_scalar(limit[:, :], iota_row[:, 0:BLOCKS - 1], float(P), float(P), ALU.mult, ALU.add))
            V.tensor_scalar(ident[:, :], iota_row[:, :], iota_col[:, :], None, ALU.is_equal)
            V.tensor_scalar(identb[:, :], iota_row[:, :], iota_col[:, :], None, ALU.is_equal).then_inc(s_const, 1)
            dve.wait_ge(s_last, 16)
            link(V.tensor_copy(last_dstf[:, :], last_dst[:, :]))
            V.tensor_tensor(below[:, :, :], last_dstf[:, :].unsqueeze(2).to_broadcast([P, VROWS, BLOCKS - 1]),
                            limit[:, :].unsqueeze(1).to_broadcast([P, VROWS, BLOCKS - 1]), ALU.is_lt).then_inc(s_below, 1)
            dve.wait_ge(s_left, 1)
            link(V.tensor_tensor(leave[:, :], bank(4)[0:BLOCKS - 1, 0:1], iota_col[0:BLOCKS - 1, :], ALU.add))
            V.tensor_scalar(passed[:, :], iota_visit[0:BLOCKS - 1, :], leave[:, :], None, ALU.is_gt).then_inc(s_passed, 1)
            dve.wait_ge(s_blk, 1)
            link(V.tensor_scalar(block_first[:, :], bank(5)[:, 0:VROWS], float(P), None, ALU.mult))
            link(V.tensor_tensor(tile_f[:, :], visit_col[:, :], bank(5)[:, 0:VROWS], ALU.subtract))
            V.tensor_copy(tile_i[:, :], tile_f[:, :]).then_inc(s_tile, 1)
            V.tensor_scalar(visit_off[:, 0:BANK], bank(6)[0:1, :], float(P), None, ALU.mult)
            V.tensor_scalar(visit_off[:, BANK:VPAD], bank(7)[0:1, 0:VPAD - BANK], float(P), None, ALU.mult).then_inc(s_off, 1)
            dve.wait_ge(s_b, 16 * 7)
            V.tensor_tensor(brz[:, :], bih[:, 0:2], bhh[:, 0:2], ALU.add)
            for b in range(BLOCKS):
                dve.wait_ge(s_qkv, b + 1)
                ps = bank(b % 4, 3 * D)
                V.tensor_tensor(q_nat[:, b * P:(b + 1) * P], ps[:, 0:D], bqkv_b[:, 0:D], ALU.add)
                V.tensor_tensor(kv_st[:, b * 2 * D:(b + 1) * 2 * D], ps[:, D:3 * D], bqkv_b[:, D:3 * D], ALU.add).then_inc(s_qkvc, 1)
            dve.wait_ge(s_ve, 16 * VROWS)
            link(V.tensor_copy(dst_v, visit_edges[:, :, 1, :]))
            V.tensor_copy(src_v, visit_edges[:, :, 0, :])
            V.tensor_copy(key_v, visit_edges[:, :, 2, :])
            link(V.tensor_tensor(rel_v, dst_v, block_first[:, :].unsqueeze(2).to_broadcast([P, VROWS, P]), ALU.subtract))
            link(V.tensor_scalar(ge0_v, rel_v, 0.0, None, ALU.is_ge))
            link(V.scalar_tensor_tensor(out=pair_v, in0=src_v, scalar=float(TYPES), in1=key_v, op0=ALU.mult, op1=ALU.add))
            link(V.scalar_tensor_tensor(out=ge0_v, in0=rel_v, scalar=float(P), in1=ge0_v, op0=ALU.is_lt, op1=ALU.mult))
            V.scalar_tensor_tensor(out=key_v, in0=dst_v, scalar=1.0, in1=ge0_v, op0=ALU.add, op1=ALU.mult).then_inc(s_vf, 1)
            for part, (r0, nr) in enumerate(FIELD_PARTS):
                dve.wait_ge(s_vt, part + 1)
                n = min(nr * P, VISITS - r0 * P)
                V.tensor_copy(rel[:, r0 * P:r0 * P + nr * P], bank(4, nr * P))
                V.tensor_copy(key[:, VPC + r0 * P:VPC + r0 * P + n], bank(5, n))
                V.tensor_copy(src_i[:, r0 * P:r0 * P + nr * P], bank(6, nr * P))
                V.tensor_copy(pair_i[:, r0 * P:r0 * P + nr * P], bank(7, nr * P)).then_inc(s_vfree, 1)
            dve.wait_ge(s_vfree, len(FIELD_PARTS))
            V.tensor_copy(pair_i[:, VISITS:VISITS + TURN], pair_i[:, 0:TURN]).then_inc(s_vi, 1)

            def build_onehot(to, v):
                return V.tensor_tensor(to, rel[:, bass.ds(v, GRP)].unsqueeze(2).to_broadcast([P, GRP, P]),
                                       iota_row[:, :].unsqueeze(1).to_broadcast([P, GRP, P]), ALU.is_equal)

            dve.wait_ge(s_kvd, 16 * len(X_BATCHES))
            dve.sem_inc(s_gfree, GROUPS)
            lc = Chain(dve, "dve_score_chain")
            with dve.Fori(0, TURNS) as i:
                lc.turn(i, GROUPS)
                for g in range(GROUPS):
                    build_onehot(onehot_b[:, g, :, :], i * TURN + g * GRP).then_inc(s_oh, 1)
                    dve.wait_ge(s_qe, i * GROUPS + g + 1)
                    dve.wait_ge(s_g[g], 16 * GRP * (i + 1))
                    p = prod[:, g % 2, :]
                    lc.link(V.tensor_tensor(p.rearrange("p (j c) -> p j c", j=GRP), kv_g[:, g, :, 0:D],
                                            bank(2 + g % 2).rearrange("p (j c) -> p j c", j=GRP), ALU.mult))
                    dve.nop(nofuse=True)
                    V.tensor_reduce(scores[:, bass.ds(i * TURN + g * GRP, GRP), :],
                                    p.rearrange("p (j h c) -> p j h c", j=GRP, h=HEADS), AX, ALU.add).then_inc(s_gfree, 1)

            for g in range(GROUPS):
                dve.wait_ge(s_vsp[g], 16 * (TURNS + 1))
            dve.wait_ge(s_gfree, GROUPS * (TURNS + 1))
            V.tensor_copy(seq_b[:, 0:SEQ].rearrange("p (g c h) -> p g c h", c=CHUNKS, h=HEADS),
                          scores[:, :, :].rearrange("p (c g) h -> p g c h", g=VPC)).then_inc(s_scx, 1)
            for n in range(len(G_BATCHES) + 1):
                dve.wait_ge(s_keyT, n + 1)
                if n < len(G_BATCHES):
                    g0, ng = G_BATCHES[n]
                    V.tensor_copy(seq_a[:, 1 + g0 * P:1 + (g0 + ng) * P], bank(n % 2, ng * P)).then_inc(s_keyTc, 1)
                else:
                    V.tensor_copy(seq_a[:, 0:1], bank(n % 2)[:, 0:1])
                    link(V.tensor_copy(seq_a[:, SEQ + 1:SEQ + 2], bank(n % 2)[:, 1:2]))
            link(V.tensor_tensor(seq_r[:, 0:SEQ + 1], seq_a[:, 1:SEQ + 2], seq_a[:, 0:SEQ + 1], ALU.not_equal))
            link(V.tensor_scalar(seq_r[:, 0:SEQ + 1], seq_r[:, 0:SEQ + 1], -BIG, None, ALU.mult))
            for n, (g0, ng) in enumerate(G_BATCHES):
                dve.wait_ge(s_scT, n + 1)
                ins = V.tensor_copy(seq_s[:, g0 * P:(g0 + ng) * P], bank(2 + n % 2, ng * P))
                ins.then_inc(s_scTc, 1)
            dve.wait_ge(s_scTc, len(G_BATCHES))

            scans = [0]

            def scan(data, to, reverse, op0, op1, initial):
                reset = seq_r[:, 1:SEQ + 1] if reverse else seq_r[:, 0:SEQ]
                data, to = data[:, 0:SEQ], to[:, 0:SEQ]
                if reverse:
                    data, to, reset = data[:, ::-1], to[:, ::-1], reset[:, ::-1]
                link(V.tensor_tensor_scan(to, reset, data, initial, op0, op1))

            def full_scan(data, to, scratch, reverse, op0, op1, start):
                scan(data, scratch, reverse, op0, op1, start)
                end = 0 if reverse else SEQ - 1
                V.tensor_copy(col_last[:, :], scratch[:, end:end + 1])
                span = seq_r[:, 1:SEQ + 1] if reverse else seq_r[:, 0:SEQ]
                V.tensor_reduce(col_pass[:, :], span, AX, ALU.min).then_inc(s_cols, 1)
                scans[0] += 1
                n = scans[0]
                dve.wait_ge(s_cr, n)
                swap = "a (c h) -> a h c"
                V.tensor_copy(row_last[:, :].rearrange("a (h c) -> a h c", h=HEADS), bank(4)[0:1, 0:P].rearrange(swap, h=HEADS))
                link(V.tensor_copy(row_pass[:, :].rearrange("a (h c) -> a h c", h=HEADS), bank(5)[0:1, 0:P].rearrange(swap, h=HEADS)))
                rows = [row_end[:, :], row_pass[:, :], row_last[:, :]]
                if reverse:
                    rows = [r[:, ::-1] for r in rows]
                link(V.tensor_tensor_scan(rows[0], rows[1], rows[2], start, op0, op1))
                ends = row_end[:, :].rearrange("a (h c) -> a c h", h=HEADS)
                carry = row_carry[:, :].rearrange("a (c h) -> a c h", h=HEADS)
                if reverse:
                    V.tensor_copy(carry[:, 0:CHUNKS - 1, :], ends[:, 1:CHUNKS, :]).then_inc(s_crc, 1)
                else:
                    V.tensor_copy(carry[:, 1:CHUNKS, :], ends[:, 0:CHUNKS - 1, :]).then_inc(s_crc, 1)
                dve.wait_ge(s_cc, n)
                link(V.tensor_copy(col_carry[:, :], bank(6)[:, 0:1]))
                scan(data, to, reverse, op0, op1, col_carry[:, :])

            full_scan(seq_s, seq_a, seq_b, False, ALU.add, ALU.max, -BIG)
            full_scan(seq_a, seq_b, seq_b, True, ALU.add, ALU.max, -BIG)
            V.tensor_tensor(seq_s[:, 0:SEQ], seq_s[:, 0:SEQ], seq_b[:, 0:SEQ], ALU.subtract).then_inc(s_sub, 1)
            link(V.tensor_scalar(seq_r[:, 0:SEQ + 1], seq_r[:, 0:SEQ + 1], 0.0, None, ALU.is_equal))
            link(V.memset(row_carry[:, :], 0.0))
            dve.wait_ge(s_exp, 1)
            full_scan(seq_s, seq_a, seq_b, False, ALU.mult, ALU.add, 0.0)
            full_scan(seq_a, seq_b, seq_b, True, ALU.mult, ALU.max, 0.0)
            link(V.reciprocal(seq_a[:, 0:SEQ], seq_b[:, 0:SEQ]))
            V.tensor_tensor(seq_s[:, 0:SEQ], seq_s[:, 0:SEQ], seq_a[:, 0:SEQ], ALU.mult).then_inc(s_alpha, 1)

            dve.wait_ge(s_alT, len(G_BATCHES))
            V.memset(x_again[:, full:full + D], 0.0).then_inc(s_xpad, 1)
            dve.wait_ge(s_alc, len(G_BATCHES))
            dve.sem_inc(s_av, GROUPS)
            with dve.Fori(0, TURNS) as i:
                for g in range(GROUPS):
                    dve.wait_ge(s_sum, i * GROUPS + g + 1)
                    dve.nop(nofuse=True)
                    build_onehot(onehot[:, g, :, :], i * TURN + g * GRP)
                    dve.wait_ge(s_vin[g], 16 * (i + 1))
                    dve.nop(nofuse=True)
                    V.tensor_tensor(av[:, g, :, :].rearrange("p j (h c) -> p j h c", h=HEADS),
                                    g_ring[:, g, :, :].rearrange("p j (h c) -> p j h c", h=HEADS),
                                    scores[:, bass.ds(i * TURN + g * GRP, GRP), :].unsqueeze(3).to_broadcast([P, GRP, HEADS, DK]),
                                    ALU.mult).then_inc(s_av, 1)
            dve.wait_ge(s_x2, 32)
            link(V.tensor_tensor(x_again.rearrange("p (b c) -> p b c", c=D), x_again.rearrange("p (b c) -> p b c", c=D),
                                 bo_b[:, :].unsqueeze(1).to_broadcast([P, BLOCKS, D]), ALU.add))
            for n, (b0, nb) in enumerate(X_BATCHES):
                dve.wait_ge(s_o, n + 1)
                link(V.tensor_tensor(x_again[:, b0 * P:(b0 + nb) * P], x_again[:, b0 * P:(b0 + nb) * P], bank(n, nb * P), ALU.add))

            def layernorm(frm, centred, to, turn):
                def nodes(a):
                    return a.rearrange("p (b c) -> p b c", c=D)
                link(V.tensor_reduce(ln_sum[:, :], nodes(frm), AX, ALU.add))
                link(V.tensor_scalar(ln_sum[:, :], ln_sum[:, :], 1.0 / D, None, ALU.mult))
                V.tensor_tensor(nodes(centred), nodes(frm), ln_sum[:, :].unsqueeze(2).to_broadcast([P, BLOCKS, D]),
                                ALU.subtract).then_inc(s_lnv, 1)
                dve.wait_ge(s_sq, turn)
                V.tensor_reduce(ln_sum[:, :], nodes(hT), AX, ALU.add).then_inc(s_lnc, 1)
                dve.wait_ge(s_lnr, turn)
                link(V.reciprocal(ln_sum[:, :], ln_var[:, :]))
                return V.tensor_tensor(nodes(to), nodes(centred), ln_sum[:, :].unsqueeze(2).to_broadcast([P, BLOCKS, D]), ALU.mult)

            layernorm(x_again, x1, x1, 1).then_inc(s_x1, 1)

            gc = Chain(dve, "dve_gru_chain")
            for k in range(4):
                dve.sem_inc(s_md[k], 16)
            with dve.Fori(0, STEPS) as s:
                for b in range(BLOCKS):
                    dve.wait_ge(s_m, s * BLOCKS + b + 1)
                    dve.wait_ge(s_md[b % 4], 16 * (s * len(range(b % 4, BLOCKS, 4)) + b // 4 + 1))
                    V.tensor_tensor(msg_st[:, b % 4, :], bank(b % 4), bmsg_b[:, :], ALU.add).then_inc(s_mc, 1)
                with dve.Fori(0, TURNS) as i:
                    for g in range(GROUPS):
                        dve.wait_ge(s_msum, (s * TURNS + i) * GROUPS + g + 1)
                        dve.nop(nofuse=True)
                        build_onehot(onehot[:, g, :, :], i * TURN + g * GRP).then_inc(s_moh, 1)
                dve.wait_ge(s_msum, GROUPS * TURNS * (s + 1) + GROUPS)
                for k in (1, 3, 5):
                    a, n = CH[k]
                    V.tensor_copy(sumT[:, a:a + n], bank(k, n)).then_inc(s_sumV, 1)
                gc.turn(s, 3 * len(CH))
                for k, (a, n) in enumerate(CH):
                    p = k % 2
                    r, z, t, h = gates[:, p, 0, 0:n], gates[:, p, 1, 0:n], gates[:, p, 2, 0:n], hT[:, a:a + n]
                    dve.wait_ge(s_rz, s * len(CH) + k + 1)
                    gc.link(V.scalar_tensor_tensor(out=t, in0=bank(4 * p + 3, n), scalar=bhh[:, 2:3], in1=r, op0=ALU.add, op1=ALU.mult))
                    V.tensor_tensor(t, t, bank(4 * p + 2, n), ALU.add).then_inc(s_npre, 1)
                    dve.wait_ge(s_tanh, s * len(CH) + k + 1)
                    gc.link(V.tensor_tensor(h, h, t, ALU.subtract))
                    gc.link(V.tensor_tensor(h, h, z, ALU.mult))
                    V.tensor_tensor(h, h, t, ALU.add).then_inc(s_h, 1)
            for n, (b0, nb) in enumerate(X_BATCHES):
                dve.wait_ge(s_fin, n + 1)
                link(V.tensor_tensor(x1[:, b0 * P:(b0 + nb) * P], x1[:, b0 * P:(b0 + nb) * P], bank(n % 8, nb * P), ALU.add))
            layernorm(x1, x_again, x_again, 2).then_inc(s_y, 1)

        @block.tensor
        def _(pe):
            T = nc.tensor

            def tr(to, frm, k=P, idn=None):
                return T.transpose(to, frm, (ident if idn is None else idn)[0:k, 0:k])

            pe.wait_ge(s_const, 1)
            pe.wait_ge(s_w, 16 * NW)
            for n, (k0, nk) in enumerate(W_BATCHES):
                if n >= 2:
                    pe.wait_ge(s_wc, n - 1)
                for k in range(k0, k0 + nk):
                    last = tr(bank(n % 2)[:, (k - k0) * D:(k - k0 + 1) * D], w_nat[:, k, :])
                last.then_inc(s_wt, 1)
            pe.wait_ge(s_x, 32)
            for n, (b0, nb) in enumerate(X_BATCHES):
                if n >= 2:
                    pe.wait_ge(s_xc, n - 1)
                for b in range(b0, b0 + nb):
                    last = tr(bank(2 + n % 2)[:, (b - b0) * P:(b - b0 + 1) * P], x_nat[:, b * P:(b + 1) * P])
                last.then_inc(s_xt, 1)
            pe.wait_ge(s_below, 1)
            for r in range(VROWS):
                last = T.matmul(bank(4)[0:BLOCKS - 1, 0:1], lhsT=below[:, r, :], rhs=ones[:, 0:1], start=(r == 0), stop=(r == VROWS - 1))
            last.then_inc(s_left, 1)
            pe.wait_ge(s_passed, 1)
            for r in range(VROWS):
                T.matmul(bank(5)[:, r:r + 1], lhsT=passed[:, r * P:(r + 1) * P], rhs=ones[0:BLOCKS - 1, 0:1], start=True, stop=True)
            T.matmul(bank(6)[0:1, :], lhsT=ones[0:BLOCKS - 1, 0:1], rhs=passed[:, 0:BANK], start=True, stop=True)
            T.matmul(bank(7)[0:1, 0:VPAD - BANK], lhsT=ones[0:BLOCKS - 1, 0:1], rhs=passed[:, BANK:VPAD], start=True, stop=True).then_inc(s_blk, 1)
            pe.wait_ge(s_wc, len(W_BATCHES))
            pe.wait_ge(s_xc, len(X_BATCHES))
            for b in range(BLOCKS):
                if b >= 4:
                    pe.wait_ge(s_qkvc, b - 3)
                T.matmul(bank(b % 4, 3 * D), lhsT=xT[:, b * P:(b + 1) * P], rhs=wqkvT[:, :], start=True, stop=True).then_inc(s_qkv, 1)
            pe.wait_ge(s_vf, 1)
            pe.wait_ge(s_off, 1)
            for part, (r0, nr) in enumerate(FIELD_PARTS):
                if part:
                    pe.wait_ge(s_vfree, part)
                for k, field in enumerate((rel_v, key_v, src_v, pair_v)):
                    for r in range(r0, r0 + nr):
                        last = tr(bank(4 + k)[:, (r - r0) * P:(r - r0 + 1) * P], field[:, r, :])
                last.then_inc(s_vt, 1)

            def offsets(turn):
                _, vals = nc.values_load_multi_w_load_instructions(
                    visit_off[0:1, bass.ds(turn * TURN, TURN)], engines=(mybir.EngineType.PE,),
                    min_val=0, max_val=PADN - P)
                return vals

            pe.wait_ge(s_qkvc, BLOCKS)
            pe.wait_ge(s_vi, 1)
            with pe.Fori(0, TURNS) as i:
                off = offsets(i)
                for g in range(GROUPS):
                    pe.wait_ge(s_oh, i * GROUPS + g + 1)
                    for j in range(GRP):
                        last = tr(bank(g % 2).bitcast(bf16)[:, j * P:(j + 1) * P], onehot_b[:, g, j, :], idn=identb)
                    last.then_inc(s_oht, 1)
                    pe.wait_ge(s_ohtc, i * GROUPS + g + 1)
                    pe.wait_ge(s_gfree, i * GROUPS + g + GROUPS - 1)
                    for j in range(GRP):
                        last = T.matmul(bank(2 + g % 2)[:, j * P:(j + 1) * P], lhsT=onehotT[:, g, j, :],
                                        rhs=q_nat[:, bass.ds(off[g * GRP + j], P)], start=True, stop=True)
                    last.then_inc(s_qe, 1)

            pe.wait_ge(s_keyx, 1)
            for n in range(len(G_BATCHES) + 1):
                if n >= 2:
                    pe.wait_ge(s_keyTc, n - 1)
                if n < len(G_BATCHES):
                    g0, ng = G_BATCHES[n]
                    for g in range(g0, g0 + ng):
                        last = tr(bank(n % 2)[:, (g - g0) * P:(g - g0 + 1) * P], seq_r[:, (g + 1) * P:(g + 2) * P])
                else:
                    T.matmul(bank(n % 2)[:, 0:1], lhsT=seq_r[:, 0:P], rhs=ident[:, P - 1:P], start=True, stop=True)
                    last = T.matmul(bank(n % 2)[:, 1:2], lhsT=seq_r[:, (VPC + 1) * P:(VPC + 2) * P], rhs=ident[:, 0:1], start=True, stop=True)
                last.then_inc(s_keyT, 1)
            pe.wait_ge(s_scx, 1)
            for n, (g0, ng) in enumerate(G_BATCHES):
                if n >= 2:
                    pe.wait_ge(s_scTc, n - 1)
                for g in range(g0, g0 + ng):
                    last = tr(bank(2 + n % 2)[:, (g - g0) * P:(g - g0 + 1) * P], seq_b[:, g * P:(g + 1) * P])
                last.then_inc(s_scT, 1)
            for n in range(1, 5):
                pe.wait_ge(s_cols, n)
                tr(bank(4)[0:1, 0:P], col_last[:, :])
                tr(bank(5)[0:1, 0:P], col_pass[:, :]).then_inc(s_cr, 1)
                pe.wait_ge(s_crc, n)
                tr(bank(6)[:, 0:1], row_carry[:, :], k=1).then_inc(s_cc, 1)
            pe.wait_ge(s_alpha, 1)
            for n, (g0, ng) in enumerate(G_BATCHES):
                if n >= 2:
                    pe.wait_ge(s_alc, n - 1)
                for g in range(g0, g0 + ng):
                    last = tr(bank(n % 2)[:, (g - g0) * P:(g - g0 + 1) * P], seq_s[:, g * P:(g + 1) * P])
                last.then_inc(s_alT, 1)

            def zero_sums():
                for k, (a, n) in enumerate(CH):
                    T.matmul(bank(k, n), lhsT=zerob[:, 0:P], rhs=zerob[:, 0:n], start=True, stop=True)

            pe.wait_ge(s_alc, len(G_BATCHES))
            zero_sums()
            pe.sem_inc(s_sum, GROUPS)
            with pe.Fori(0, TURNS) as i:
                off = offsets(i)
                for g in range(GROUPS):
                    pe.wait_ge(s_av, i * GROUPS + GROUPS + g + 1)
                    for j in range(GRP):
                        last = T.matmul(PS[:, bass.ds(off[g * GRP + j], P)], lhsT=av[:, g, j, :], rhs=onehot[:, g, j, :],
                                        start=False, stop=True, skip_group_check=True)
                    last.then_inc(s_sum, 1)
            pe.wait_ge(s_attc, len(CH))
            for n, (b0, nb) in enumerate(X_BATCHES):
                for b in range(b0, b0 + nb):
                    last = T.matmul(bank(n)[:, (b - b0) * D:(b - b0 + 1) * D], lhsT=sumT[:, b * P:(b + 1) * P], rhs=woT[:, :], start=True, stop=True)
                last.then_inc(s_o, 1)
            pe.wait_ge(s_x1, 1)
            for n, (b0, nb) in enumerate(X_BATCHES):
                if n >= 2:
                    pe.wait_ge(s_htc, n - 1)
                for b in range(b0, b0 + nb):
                    last = tr(bank(n % 2)[:, (b - b0) * P:(b - b0 + 1) * P], x1[:, b * P:(b + 1) * P])
                last.then_inc(s_ht, 1)
            pe.wait_ge(s_htc, len(X_BATCHES))
            pe.sem_inc(s_msum, GROUPS)
            pe.sem_inc(s_h, len(CH))
            with pe.Fori(0, STEPS) as s:
                pe.wait_ge(s_h, len(CH) * (s + 1))
                for b in range(BLOCKS):
                    if b >= 4:
                        pe.wait_ge(s_mc, s * BLOCKS + b - 3)
                    T.matmul(bank(b % 4), lhsT=hT[:, b * P:(b + 1) * P], rhs=wmsgT[:, :], start=True, stop=True).then_inc(s_m, 1)
                pe.wait_ge(s_mc, (s + 1) * BLOCKS)
                zero_sums()
                with pe.Fori(0, TURNS) as i:
                    off = offsets(i)
                    for g in range(GROUPS):
                        pe.wait_ge(s_moh, (s * TURNS + i) * GROUPS + g + 1)
                        pe.wait_ge(s_mg[g], 16 * GRP * (s * TURNS + i + 1))
                        for j in range(GRP):
                            last = T.matmul(PS[:, bass.ds(off[g * GRP + j], P)], lhsT=g_ring[:, g, j, :], rhs=onehot[:, g, j, :],
                                            start=False, stop=True, skip_group_check=True)
                        last.then_inc(s_msum, 1)
                pe.wait_ge(s_sumA, 4 * (s + 1))
                pe.wait_ge(s_sumV, 3 * (s + 1))
                for k, (a, n) in enumerate(CH):
                    p = 4 * (k % 2)
                    if k >= 2:
                        pe.wait_ge(s_h, len(CH) * (s + 1) + k - 1)
                    m, h = sumT[:, a:a + n], hT[:, a:a + n]
                    T.matmul(bank(p, n), lhsT=wihT[:, 0:D], rhs=m, start=True, stop=False)
                    T.matmul(bank(p, n), lhsT=whhT[:, 0:D], rhs=h, start=False, stop=True)
                    T.matmul(bank(p + 1, n), lhsT=wihT[:, D:2 * D], rhs=m, start=True, stop=False)
                    T.matmul(bank(p + 1, n), lhsT=whhT[:, D:2 * D], rhs=h, start=False, stop=True)
                    T.matmul(bank(p + 2, n), lhsT=wihT[:, 2 * D:3 * D], rhs=m, start=True, stop=True)
                    T.matmul(bank(p + 3, n), lhsT=whhT[:, 2 * D:3 * D], rhs=h, start=True, stop=True).then_inc(s_gate, 1)
            pe.wait_ge(s_h, len(CH) * (STEPS + 1))
            for n, (b0, nb) in enumerate(X_BATCHES):
                for b in range(b0, b0 + nb):
                    last = tr(bank(n)[:, (b - b0) * P:(b - b0 + 1) * P], hT[:, b * P:(b + 1) * P])
                last.then_inc(s_fin, 1)


_INS = ['x', 'src', 'dst', 'edge_type_4', 'L0_gnn_Wq', 'L0_gnn_bq', 'L0_gnn_Wk', 'L0_gnn_bk', 'L0_gnn_Wv', 'L0_gnn_bv',
        'L0_gnn_Wo', 'L0_gnn_bo', 'L1_gnn_W_msg', 'L1_gnn_b_msg', 'L1_gnn_w_ih', 'L1_gnn_w_hh', 'L1_gnn_b_ih', 'L1_gnn_b_hh']


def kernel(**inputs):
    import numpy as _np
    import concourse.bacc as _bacc
    from concourse import mybir as _mybir
    from concourse.bass_utils import run_bass_kernel_spmd as _run

    nc = _bacc.Bacc("TRN2", target_bir_lowering=False, num_devices=1)
    arrays, args = {}, []
    for name in _INS:
        a = _np.ascontiguousarray(inputs[name])
        arrays[f"in_{name}"] = a
        args.append(nc.dram_tensor(f"in_{name}", a.shape, _mybir.dt.from_np(a.dtype), kind="ExternalInput").ap())
    shape = inputs['x'].shape
    args.append(nc.dram_tensor("out_0", shape, _mybir.dt.float32, kind="ExternalOutput").ap())
    gnn_program(nc, *args)
    r = _run(nc, [arrays], core_ids=[0])
    return r.results[0]["out_0"]
```

```python
import concourse.bass as bass
from concourse import mybir
from contextlib import ExitStack


def gnn_program(nc, x, src, dst, etype, Wq, bq, Wk, bk, Wv, bv, Wo, bo, W_msg, b_msg,
                w_ih, w_hh, b_ih, b_hh, out):
    f32, bf16, i32 = mybir.dt.float32, mybir.dt.bfloat16, mybir.dt.int32
    f16, f8, u8 = mybir.dt.float16, mybir.dt.float8e4, mybir.dt.uint8
    ALU = mybir.AluOpType
    ACT = mybir.ActivationFunctionType
    AX = mybir.AxisListType.X

    P = 128
    NODES, D = x.shape
    EDGES = src.shape[0]
    HEADS = 8
    DK = D // HEADS
    TYPES = W_msg.shape[0] // D
    STEPS = 4
    EPS = 1e-5
    BIG = 1.0e30
    BLOCKS = (NODES + P - 1) // P
    PADN = BLOCKS * P
    TAILN = NODES - (BLOCKS - 1) * P
    FULLT = EDGES // P
    TAILE = EDGES - FULLT * P
    TILES = FULLT + (TAILE > 0)
    GRP, GROUPS = 4, 4
    TURN = GRP * GROUPS
    TURNS = (TILES + BLOCKS - 1 + TURN - 1) // TURN
    VISITS = TURNS * TURN
    VROWS = (VISITS + P - 1) // P
    VPAD = VROWS * P
    NO_NODE = 1 << 20
    CHUNKS = P // HEADS
    VPC = VISITS // CHUNKS
    SEQ = VPC * P
    assert CHUNKS * VPC == VISITS
    BANK = 512
    ACC_BANKS = (PADN + BANK - 1) // BANK
    WIN = 4
    PAIRS = BLOCKS * TYPES
    WCOLS = PAIRS * WIN
    WINDOWS = (NODES + WIN - 1) // WIN
    WPB = P // WIN
    WGRP = 8
    WVISITS = TURNS * GROUPS * WGRP
    assert WVISITS >= TILES + WINDOWS
    WROWS = (WVISITS + P - 1) // P
    WPAD = WROWS * P
    WK = (WINDOWS + P - 1) // P
    WSLOTS = 4
    COUNT_OFF = WSLOTS * BANK
    EXACT = 16
    EXACT_CODE = 0x58
    LO = 2048.0
    CH = [(c * BANK, min(BANK, PADN - c * BANK)) for c in range(ACC_BANKS)]

    ctx = ExitStack()
    with ctx:
        def sb(name, shape, dt):
            return ctx.enter_context(nc.sbuf_tensor(name, shape, dt))

        def sem(name):
            return ctx.enter_context(nc.semaphore(name))

        class Chain:

            def __init__(self, eng, name):
                self.eng, self.sem, self.base, self.n = eng, sem(name), 0, 0

            def turn(self, turn, per_turn):
                self.base, self.n = turn * per_turn, 0

            def link(self, instruction):
                self.n += 1
                instruction.then_inc(self.sem, 1)
                self.eng.wait_ge(self.sem, self.base + self.n)

        kv_d = nc.dram_tensor("kv_rows", [PADN, 2 * D], f32, kind="Internal").ap()
        msg_d = nc.dram_tensor("msg_rows", [PADN * TYPES, D], f32, kind="Internal").ap()
        v_d = nc.dram_tensor("v_of_visits", [P, VISITS, D], f32, kind="Internal").ap()
        edges_d = nc.dram_tensor("edge_tiles", [VPAD, 3 * P], i32, kind="Internal").ap()
        edges_v = edges_d.rearrange("t (k e) -> t k e", k=3)

        BLK_I = PAIRS * P // 4
        counts_d = nc.dram_tensor("counts", [BLOCKS * P, BLK_I], i32, kind="Internal").ap()

        PS = ctx.enter_context(nc.psum_tensor("PS", [P, 8 * BANK], f32))

        def bank(k, n=BANK):
            return PS[:, k * BANK:k * BANK + n]

        ident = sb("ident", [P, P], f32)
        identb = sb("identb", [P, P], bf16)
        iota_row = sb("iota_row", [P, P], f32)
        iota_col = sb("iota_col", [P, 1], f32)
        visit_col = sb("visit_col", [P, VROWS], f32)
        visit_i = sb("visit_i", [P, VROWS], i32)
        ones = sb("ones", [P, P], f32)
        zerob = sb("zerob", [P, BANK], bf16)
        pad_rows = sb("pad_rows", [P, 3 * P], i32)
        last_dst = sb("last_dst", [P, VROWS], i32)
        last_dstf = sb("last_dstf", [P, VROWS], f32)
        limit = sb("limit", [P, BLOCKS - 1], f32)
        below = sb("below", [P, VROWS, BLOCKS - 1], f32)
        leave = sb("leave", [BLOCKS - 1, 1], f32)
        block_first = sb("block_first", [P, VROWS], f32)
        tile_f = sb("tile_f", [P, VROWS], f32)
        tile_i = sb("tile_i", [P, VROWS], i32)
        visit_off = sb("visit_off", [1, VPAD // 4], i32)
        wvisit_col = sb("wvisit_col", [P, WROWS], f32)
        wleave = sb("wleave", [P, WK], f32)
        wleave_row = sb("wleave_row", [1, WINDOWS], i32)
        window_first = sb("window_first", [P, WROWS], f32)
        wtile_f = sb("wtile_f", [P, WROWS], f32)
        wtile_i = sb("wtile_i", [P, WROWS], i32)
        onesb = sb("onesb", [P, 1], bf16)
        cell = sb("cell", [P, WPAD], f32)
        low = sb("low", [P, WPAD], f32)
        count_sb = sb("count_sb", [P, PAIRS], f32)
        bmsg_t = sb("bmsg_t", [TYPES, D], f32)
        codes = sb("codes", [P, STEPS * ACC_BANKS], f32)
        code_max = sb("code_max", [P, 1], f32)
        flag_f = sb("flag_f", [1, 1], f32)
        flag_i = sb("flag_i", [1, 1], i32)
        rel = sb("rel", [P, VPAD], f32)
        key = sb("key", [P, VPC + VPAD + VPC], f32)
        src_i = sb("src_i", [P, VPAD], i32)
        pair_i = sb("pair_i", [P, VPAD], i32)
        stage = sb("stage", [P, GROUPS, GRP], i32)
        scores = sb("scores", [P, VISITS, HEADS], f32)
        wqkvT = sb("wqkvT", [P, 3 * D], f32)
        woT = sb("woT", [P, D], f32)
        wmsgT = sb("wmsgT", [P, TYPES * D], f32)
        wihT = sb("wihT", [P, 3 * D], f32)
        whhT = sb("whhT", [P, 3 * D], f32)
        bqkv_b = sb("bqkv_b", [P, 3 * D], f32)
        bo_b = sb("bo_b", [P, D], f32)
        bmsg_b = sb("bmsg_b", [P, TYPES * D], f32)
        bih = sb("bih", [P, 3], f32)
        bhh = sb("bhh", [P, 3], f32)
        brz = sb("brz", [P, 2], f32)
        col_last = sb("col_last", [P, 1], f32)
        col_pass = sb("col_pass", [P, 1], f32)
        col_carry = sb("col_carry", [P, 1], f32)
        row_last = sb("row_last", [1, P], f32)
        row_pass = sb("row_pass", [1, P], f32)
        row_end = sb("row_end", [1, P], f32)
        row_carry = sb("row_carry", [1, P], f32)
        ln_sum = sb("ln_sum", [P, BLOCKS], f32)
        ln_var = sb("ln_var", [P, BLOCKS], f32)
        eps_col = sb("eps_col", [P, 1], f32)

        region = sb("region", [P, 4 * (SEQ + 2 * P)], f32)
        cut_at = [0]

        def cut(n):
            cut_at[0] += n
            assert cut_at[0] <= 4 * (SEQ + 2 * P)
            return region[:, cut_at[0] - n:cut_at[0]]

        x_nat = cut(PADN)
        xT = cut(PADN)
        q_nat = cut(PADN)
        base_tables = cut_at[0]
        kv_st = cut(2 * PADN)
        visit_edges = cut(VROWS * 3 * P).bitcast(i32).rearrange("p (r k e) -> p r k e", r=VROWS, k=3)
        dst_v, rel_v, ge0_v, key_v, src_v, pair_v = (
            cut(VPAD).rearrange("p (r e) -> p r e", r=VROWS) for _ in range(6))
        w_nat = region[:, 4 * (SEQ + 2 * P) - 14 * P:4 * (SEQ + 2 * P)].rearrange("p (k c) -> p k c", k=14)
        cut_at[0] = base_tables
        iota_w = cut(WPAD)
        ints = cut(WPAD).bitcast(i32)
        limit_w = cut(WINDOWS)
        row_w = cut(WPAD)
        row_first = cut(WPAD)
        passed = cut(VPAD)[0:BLOCKS - 1, :]
        cut_at[0] += cut_at[0] % 2
        below_w = cut(WK * 2 * WINDOWS // 4 * 2).bitcast(bf16)[:, 0:VROWS * WINDOWS].rearrange("p (r w) -> p r w", r=VROWS)
        passed_w = scores[:, :, :].rearrange("p v h -> p (v h)").bitcast(bf16)[:, 0:WK * WPAD].rearrange("p (k v) -> p k v", k=WK)
        cut_at[0] = base_tables
        wedges = cut(WROWS * 3 * P).bitcast(i32).rearrange("p (r k e) -> p r k e", r=WROWS, k=3)
        wf = [cut(WPAD) for _ in range(4)]
        whi_i = wedges[:, :, 1, :]
        cut_at[0] = 0
        acc = cut(2 * BLK_I).bitcast(i32).rearrange("p (s c) -> p s c", s=2)
        cut_at[0] = base_tables
        kv_g = cut(TURN * 2 * D).rearrange("p (g j c) -> p g j c", g=GROUPS, j=GRP)
        onehot_b = cut(GROUPS * GRP * P // 2).bitcast(bf16).rearrange("p (g j e) -> p g j e", g=GROUPS, j=GRP)
        onehotT = cut(GROUPS * GRP * P).rearrange("p (g j e) -> p g j e", g=GROUPS, j=GRP)
        prod = cut(2 * GRP * D).rearrange("p (g c) -> p g c", g=2)
        cells = cut(WGRP * WCOLS // 2).bitcast(bf16).rearrange("p (s c) -> p s c", s=WGRP)
        lows = cut(WGRP * P // 2).bitcast(bf16).rearrange("p (s c) -> p s c", s=WGRP)
        iota_h = cut(WCOLS // 2).bitcast(f16)
        types_b = sb("types_b", [P, VPAD, TYPES], bf16)
        wrow = sb("wrow", [1, WPAD // 4], i32)
        cell_st = sb("cell_st", [P, 2, WGRP], f32)
        low_st = sb("low_st", [P, 2, WGRP], f32)
        cut_at[0] = 0
        seq_s, seq_r, seq_a, seq_b = (cut(SEQ + 2 * P) for _ in range(4))
        cut_at[0] = 0
        x_again = cut(PADN)
        x1 = cut(PADN)
        hT = cut(PADN)
        sumT = cut(PADN)
        base_rings = cut_at[0]
        g_ring = cut(TURN * D).rearrange("p (g j c) -> p g j c", g=GROUPS, j=GRP)
        onehot = cut(GROUPS * GRP * P).rearrange("p (g j e) -> p g j e", g=GROUPS, j=GRP)
        av = cut(TURN * D).rearrange("p (g j c) -> p g j c", g=GROUPS, j=GRP)
        msg_st = cut(4 * TYPES * D).rearrange("p (s c) -> p s c", s=4)
        cut_at[0] = base_rings
        ring = cut(4 * BLK_I).bitcast(i32)
        ring8 = ring.bitcast(f8).rearrange("p (s k c) -> p s k c", s=4, k=BLOCKS)
        ringu = ring.bitcast(u8)
        rT = cut(2 * BANK).rearrange("p (s n) -> p s n", s=2)
        gates = x_again[:, 0:2 * 3 * BANK].rearrange("p (s k n) -> p s k n", s=2, k=3)
        countT = sumT[0:TYPES, :]
        flat = scores[:, :, :].rearrange("p v h -> p (v h)")
        h_hi = flat[:, 0:PADN // 2].bitcast(f16)
        h_lo = flat[:, PADN // 2:PADN].bitcast(f16)
        s_hi = flat[:, PADN:PADN + 2 * BANK].rearrange("p (s n) -> p s n", s=2)
        sum_b = flat[:, PADN + 2 * BANK:PADN + 6 * BANK].rearrange("p (s n) -> p s n", s=4)

        s_w, s_x, s_b, s_pad, s_iota = sem("weights_in"), sem("x_in"), sem("bias_in"), sem("pad_rows_set"), sem("iota_done")
        s_edges, s_last = sem("edge_tiles_written"), sem("last_dst_in")
        s_const, s_xpad = sem("constants_set"), sem("x_padding_zeroed")
        s_wt, s_wc = sem("weights_transposed"), sem("weights_copied")
        s_xt, s_xc = sem("x_transposed"), sem("xT_copied")
        s_qkv, s_qkvc, s_kvd = sem("qkv_ready"), sem("qkv_copied"), sem("kv_rows_written")
        s_wvis, s_wfree, s_evac = sem("window_visit_done"), sem("window_onehots_built"), sem("window_counts_copied")
        s_flush = [sem(f"counts_written{k}") for k in range(2)]
        s_we, s_wff, s_wft, s_wrow = sem("window_edges_in"), sem("window_fields_ready"), sem("window_fields_transposed"), sem("window_rows_ready")
        s_wcp = sem("window_copied")
        s_ctz, s_cnt, s_ctt = sem("count_banks_zeroed"), sem("edge_counts_copied"), sem("edge_counts_transposed")
        s_ctc, s_hn, s_hh, s_hd, s_hl = sem("countT_copied"), sem("h_natural"), sem("h_high_ready"), sem("h_rest_ready"), sem("h_low_ready")
        s_cin = [sem(f"counts_loaded{k}") for k in range(4)]
        s_dense, s_chk, s_shi, s_sb = sem("block_product_done"), sem("codes_checked"), sem("high_sum_copied"), sem("block_sum_ready")
        s_r, s_rTc, s_g1, s_g2 = sem("message_sums_ready"), sem("rT_copied"), sem("gate_products_ready"), sem("i_n_product_ready")
        s_sr, s_sz, s_np, s_tn, s_hu = sem("r_gate_ready"), sem("z_gate_ready"), sem("candidate_input_ready"), sem("candidate_ready"), sem("state_updated")
        s_cm, s_cmr, s_flag, s_hfin = sem("code_max_ready"), sem("code_row_ready"), sem("flag_ready"), sem("last_h_product")
        s_fht, s_fhtc = sem("fallback_x1_transposed"), sem("fallback_hT_copied")
        s_below, s_left, s_passed, s_blk = sem("below_ready"), sem("tiles_before_ready"), sem("passed_ready"), sem("visit_blocks_ready")
        s_tile, s_ve, s_vf, s_vt = sem("visit_tiles_ready"), sem("visit_edges_in"), sem("visit_fields_ready"), sem("fields_transposed")
        s_vfree, s_vi, s_off = sem("field_bank_free"), sem("visit_arrays_ready"), sem("visit_offsets_ready")
        s_g = [sem(f"kv_gathered{g}") for g in range(GROUPS)]
        s_stage, s_gfree = sem("indices_staged"), sem("kv_group_scored")
        s_vsp = [sem(f"v_spilled{g}") for g in range(GROUPS)]
        s_oh, s_oht, s_ohtc, s_qe, s_pr = sem("onehot_built"), sem("onehot_transposed"), sem("onehotT_copied"), sem("q_of_edges_ready"), sem("q_bank_read")
        s_keyx, s_scx = sem("keys_spread"), sem("scores_spread")
        s_keyT, s_keyTc, s_scT, s_scTc = sem("key_transposed"), sem("keyT_copied"), sem("score_transposed"), sem("scoreT_copied")
        s_cr, s_crc, s_cc = sem("carry_rows_ready"), sem("carry_row_set"), sem("carry_column_ready")
        s_cols, s_sub, s_exp = sem("carry_inputs_set"), sem("score_less_max"), sem("exp_done")
        s_alpha, s_alT, s_alc = sem("alpha_ready"), sem("alpha_transposed"), sem("alpha_copied")
        s_vin = [sem(f"v_loaded{g}") for g in range(GROUPS)]
        s_av, s_sum = sem("weighted_v_ready"), sem("att_group_summed")
        s_zero = sem("sum_banks_zeroed")
        s_attc, s_o, s_x2, s_res = sem("att_copied"), sem("o_product_ready"), sem("x_again_in"), sem("residual_ready")
        s_lnv, s_lnr, s_lnc, s_sq = sem("ln_centred"), sem("ln_root"), sem("ln_varsum"), sem("ln_squared")
        s_x1, s_ht, s_htc = sem("x1_ready"), sem("x1_transposed"), sem("hT_copied")
        s_m, s_mc = sem("messages_ready"), sem("messages_copied")
        s_md = [sem(f"msg_rows_written{k}") for k in range(4)]
        s_mg = [sem(f"msg_gathered{g}") for g in range(GROUPS)]
        s_mstage, s_moh, s_msum = sem("msg_indices_staged"), sem("msg_onehot_built"), sem("msg_group_summed")
        s_sumA, s_sumV = sem("sum_copied_act"), sem("sum_copied_dve")
        s_gate, s_rz, s_npre, s_tanh, s_h = sem("gates_ready"), sem("rz_ready"), sem("n_input_ready"), sem("tanh_ready"), sem("h_updated")
        s_fin, s_y, s_out = sem("h_transposed"), sem("y_ready"), sem("out_written")

        block = ctx.enter_context(nc.Block())
        weights = ([Wq, Wk, Wv, Wo] + [W_msg[k * D:(k + 1) * D, :] for k in range(TYPES)]
                   + [w_ih[k * D:(k + 1) * D, :] for k in range(3)] + [w_hh[k * D:(k + 1) * D, :] for k in range(3)])
        NW = len(weights)
        wT = ([wqkvT[:, k * D:(k + 1) * D] for k in range(3)] + [woT[:, :]]
              + [wmsgT[:, k * D:(k + 1) * D] for k in range(TYPES)]
              + [wihT[:, k * D:(k + 1) * D] for k in range(3)] + [whhT[:, k * D:(k + 1) * D] for k in range(3)])
        W_BATCHES = [(k, min(4, NW - k)) for k in range(0, NW, 4)]
        X_BATCHES = [(k, min(4, BLOCKS - k)) for k in range(0, BLOCKS, 4)]
        G_BATCHES = [(k, min(4, VPC - k)) for k in range(0, VPC, 4)]
        FIELD_PARTS = [(0, 4), (4, VROWS - 4)]
        biases = ([(bqkv_b[:, k * D:(k + 1) * D], b) for k, b in enumerate((bq, bk, bv))]
                  + [(bo_b[:, :], bo), (bmsg_b[:, :], b_msg)])

        def flag_value(eng):
            return eng.value_load(flag_i[0:1, 0:1], min_val=0, max_val=1)

        def psT(g):
            return bank(5).bitcast(bf16)[:, (g % 2) * BANK:(g % 2 + 1) * BANK]

        @block.sync
        def _(sp):
            sp.wait_ge(s_pad, 2)
            for k, a in enumerate((src, dst, etype)):
                sp.dma_start(edges_v[0:FULLT, k, :], a[0:FULLT * P].rearrange("(t e) -> t e", e=P)).then_inc(s_edges, 16)
                sp.dma_start(edges_v[FULLT:TILES, k, 0:TAILE], a[FULLT * P:EDGES].rearrange("(t e) -> t e", t=1)).then_inc(s_edges, 16)
                sp.dma_start(edges_v[FULLT:TILES, k, TAILE:P], pad_rows[0:1, k * P + TAILE:(k + 1) * P]).then_inc(s_edges, 16)
            sp.dma_start(edges_d[TILES:VPAD, :], pad_rows[0:VPAD - TILES, :]).then_inc(s_edges, 16)
            for k, w in enumerate(weights):
                sp.dma_start(w_nat[:, k, :], w).then_inc(s_w, 16)
            sp.wait_ge(s_xpad, 1)
            full = (BLOCKS - 1) * P
            sp.dma_start(x_nat[:, 0:full].rearrange("p (b c) -> p b c", c=D),
                         x[0:full, :].rearrange("(b p) c -> p b c", p=P)).then_inc(s_x, 16)
            sp.dma_start(x_nat[0:TAILN, full:full + D], x[full:NODES, :]).then_inc(s_x, 16)
            for to, b in biases:
                sp.dma_start(to, b.rearrange("(a n) -> a n", a=1).broadcast_to([P, b.shape[0]])).then_inc(s_b, 16)
            for to, b in ((bih, b_ih), (bhh, b_hh)):
                with nc.allow_non_contiguous_dma(reason="a few hundred bias elements"):
                    sp.dma_start(to[:, :], b.rearrange("(k p) -> p k", p=P)).then_inc(s_b, 16)
            sp.wait_ge(s_edges, 16 * 10)
            with nc.allow_non_contiguous_dma(reason="one element of each tile"):
                sp.dma_start(last_dst[:, :], edges_d.rearrange("(r p) c -> p r c", p=P)[:, :, 2 * P - 1:2 * P].rearrange("p r c -> p (r c)")).then_inc(s_last, 16)
            sp.dma_start(bmsg_t[:, :], b_msg.rearrange("(t f) -> t f", t=TYPES)).then_inc(s_b, 16)
            for n, (b0, nb) in enumerate(X_BATCHES):
                sp.wait_ge(s_qkvc, b0 + nb)
                sp.dma_start(kv_d[b0 * P:(b0 + nb) * P, :].rearrange("(b p) c -> p b c", p=P),
                             kv_st[:, b0 * 2 * D:(b0 + nb) * 2 * D].rearrange("p (b c) -> p b c", b=nb)).then_inc(s_kvd, 16)
            for g in range(GROUPS):
                sp.sem_inc(s_vsp[g], 16)
            with sp.Fori(0, TURNS) as i:
                for g in range(GROUPS):
                    sp.wait_ge(s_g[g], 16 * GRP * (i + 1))
                    sp.dma_start(v_d[:, bass.ds(i * TURN + g * GRP, GRP), :], kv_g[:, g, :, D:2 * D]).then_inc(s_vsp[g], 16)
            sp.wait_ge(s_alT, len(G_BATCHES))
            sp.wait_ge(s_xpad, 2)
            sp.dma_start(x_again[:, 0:full].rearrange("p (b c) -> p b c", c=D),
                         x[0:full, :].rearrange("(b p) c -> p b c", p=P)).then_inc(s_x2, 16)
            sp.dma_start(x_again[0:TAILN, full:full + D], x[full:NODES, :]).then_inc(s_x2, 16)
            for g in range(GROUPS):
                sp.wait_ge(s_vsp[g], 16 * (TURNS + 1))
            with sp.Fori(0, TURNS) as i:
                for g in range(GROUPS):
                    sp.wait_ge(s_av, i * GROUPS + g + 1)
                    sp.dma_start(g_ring[:, g, :, :], v_d[:, bass.ds(i * TURN + g * GRP, GRP), :]).then_inc(s_vin[g], 16)
            for k in range(2):
                sp.wait_ge(s_flush[k], 16 * (BLOCKS // 2 + (k < BLOCKS % 2) + 1))
            sp.wait_ge(s_attc, len(CH))
            last_chunk = ACC_BANKS - 1
            cd = counts_d.rearrange("(b p) c -> p b c", p=P)
            with sp.Fori(0, STEPS) as s:
                sp.wait_ge(s_dense, s * BLOCKS + 4)
                sp.nop(nofuse=True)
                with sp.Fori(0, last_chunk) as c:
                    for k in range(4):
                        sp.wait_ge(s_dense, s * BLOCKS + c * 4 + k + 1)
                        sp.wait_ge(s_chk, s * ACC_BANKS + c + 1)
                        sp.dma_start(ring[:, k * BLK_I:(k + 1) * BLK_I], cd[:, bass.ds(c * 4 + k, 1), :].rearrange("p b c -> p (b c)")).then_inc(s_cin[k], 16)
                sp.wait_ge(s_dense, s * BLOCKS + last_chunk * 4 + 1)
                sp.wait_ge(s_chk, s * ACC_BANKS + last_chunk + 1)
                sp.dma_start(ring[:, 0:BLK_I], cd[:, BLOCKS - 1, :]).then_inc(s_cin[0], 16)
            sp.wait_ge(s_flag, 1)
            with sp.If(flag_value(sp) > 0):
                with sp.Fori(0, STEPS) as s:
                    for b in range(BLOCKS):
                        sp.wait_ge(s_mc, s * BLOCKS + b + 1)
                        sp.dma_start(msg_d[b * P * TYPES:(b + 1) * P * TYPES, :].rearrange("(p t) c -> p (t c)", p=P),
                                     msg_st[:, b % 4, :]).then_inc(s_md[b % 4], 16)
            sp.wait_ge(s_y, 1)
            sp.dma_start(out[0:full, :].rearrange("(b p) c -> p b c", p=P),
                         x_again[:, 0:full].rearrange("p (b c) -> p b c", c=D)).then_inc(s_out, 16)
            sp.dma_start(out[full:NODES, :], x_again[0:TAILN, full:full + D]).then_inc(s_out, 16)
            sp.wait_ge(s_out, 32)

        @block.gpsimd
        def _(pool):
            ch = Chain(pool, "pool_chain")
            ch.link(nc.gpsimd.memset(pad_rows[:, :], 0))
            nc.gpsimd.memset(pad_rows[:, P:2 * P], NO_NODE).then_inc(s_pad, 2)
            nc.gpsimd.iota(ints, [[1, WPAD]], base=0, channel_multiplier=0).then_inc(s_iota, 1)
            nc.gpsimd.iota(wtile_i[:, :], [[P, WROWS]], base=0, channel_multiplier=1).then_inc(s_iota, 1)
            nc.gpsimd.iota(visit_i[:, :], [[P, VROWS]], base=0, channel_multiplier=1).then_inc(s_iota, 1)
            pool.wait_ge(s_edges, 16 * 10)
            pool.wait_ge(s_tile, 1)
            for r in range(WROWS):
                nc.gpsimd.indirect_dma_start(
                    out=wedges[:, r, :, :].rearrange("p k e -> p (k e)"), out_offset=None, in_=edges_d[:, :],
                    in_offset=bass.IndirectOffsetOnAxis(ap=wtile_i[:, r:r + 1], axis=0)).then_inc(s_we, 16)
            pool.wait_ge(s_wft, 2)
            for r in range(VROWS):
                nc.gpsimd.indirect_dma_start(
                    out=visit_edges[:, r, :, :].rearrange("p k e -> p (k e)"), out_offset=None, in_=edges_d[:, :],
                    in_offset=bass.IndirectOffsetOnAxis(ap=tile_i[:, r:r + 1], axis=0)).then_inc(s_ve, 16)
            pool.wait_ge(s_kvd, 16 * len(X_BATCHES))
            pool.wait_ge(s_vt, 2)
            with pool.Fori(0, TURNS) as i:
                for g in range(GROUPS):
                    pool.wait_ge(s_gfree, i * GROUPS + g + 1)
                    pool.wait_ge(s_vsp[g], 16 * (i + 1))
                    pool.wait_ge(s_stage, i * GROUPS + g + 1)
                    pool.nop(nofuse=True)
                    for j in range(GRP):
                        nc.gpsimd.indirect_dma_start(
                            out=kv_g[:, g, j, :], out_offset=None, in_=kv_d[:, :],
                            in_offset=bass.IndirectOffsetOnAxis(ap=stage[:, g, j:j + 1], axis=0)).then_inc(s_g[g], 16)
            pool.wait_ge(s_flag, 1)
            with pool.If(flag_value(pool) > 0):
                with pool.Fori(0, STEPS) as s:
                    for k in range(4):
                        pool.wait_ge(s_md[k], 16 * len(range(k, BLOCKS, 4)) * (s + 1) + 16)
                    pool.nop(nofuse=True)
                    with pool.Fori(0, TURNS) as i:
                        for g in range(GROUPS):
                            pool.wait_ge(s_msum, (s * TURNS + i) * GROUPS + g + 1)
                            pool.wait_ge(s_mstage, (s * TURNS + i) * GROUPS + g + 1)
                            pool.nop(nofuse=True)
                            for j in range(GRP):
                                nc.gpsimd.indirect_dma_start(
                                    out=g_ring[:, g, j, :], out_offset=None, in_=msg_d[:, :],
                                    in_offset=bass.IndirectOffsetOnAxis(ap=stage[:, g, j:j + 1], axis=0)).then_inc(s_mg[g], 16)

        @block.scalar
        def _(act):
            ch = Chain(act, "act_chain")
            for n, (k0, nk) in enumerate(W_BATCHES):
                act.wait_ge(s_wt, n + 1)
                for k in range(k0, k0 + nk):
                    last = nc.scalar.copy(wT[k], bank(n % 2)[:, (k - k0) * D:(k - k0 + 1) * D])
                last.then_inc(s_wc, 1)
            for n, (b0, nb) in enumerate(X_BATCHES):
                act.wait_ge(s_xt, n + 1)
                nc.scalar.copy(xT[:, b0 * P:(b0 + nb) * P], bank(2 + n % 2)[:, 0:nb * P]).then_inc(s_xc, 1)

            act.wait_ge(s_vi, 1)
            act.wait_ge(s_qkv, BLOCKS)
            act.wait_ge(s_ctz, 1)
            act.sem_inc(s_evac, WSLOTS)
            for k in range(2):
                act.sem_inc(s_flush[k], 16)

            def copy_windows(first, windows, slot):
                _, left = nc.values_load_multi_w_load_instructions(
                    wleave_row[0:1, bass.ds(first, windows)], engines=(mybir.EngineType.Activation,), min_val=1, max_val=WPAD + WGRP)
                to = acc[:, slot, :].bitcast(f8).rearrange("p (j n) -> p j n", j=PAIRS)
                for w in range(windows):
                    act.wait_ge(s_wvis, left[w])
                    act.nop(nofuse=True)
                    nc.scalar.copy(to[:, :, w * WIN:(w + 1) * WIN],
                                   bank(w % WSLOTS, WCOLS).rearrange("p (j n) -> p j n", j=PAIRS), saturate=False).then_inc(s_wcp, 1)
                    act.wait_ge(s_wcp, first + w + 1)
                    nc.scalar.copy(bank(w % WSLOTS, WCOLS), zerob[:, 0:WCOLS]).then_inc(s_evac, 1)

            with act.Fori(0, BLOCKS // 2) as i:
                for k in range(2):
                    act.wait_ge(s_flush[k], 16 * (i + 1))
                    act.nop(nofuse=True)
                    copy_windows(i * (2 * WPB) + k * WPB, WPB, k)
                    act.wait_ge(s_evac, WSLOTS + i * (2 * WPB) + (k + 1) * WPB)
                    act.nop(nofuse=True)
                    act.dma_start(counts_d[bass.ds((i * 2 + k) * P, P), :], acc[:, k, :]).then_inc(s_flush[k], 16)
            rest = WINDOWS - (BLOCKS - 1) * WPB
            act.wait_ge(s_flush[0], 16 * (BLOCKS // 2 + 1))
            nc.scalar.copy(acc[:, 0, :].bitcast(f8).rearrange("p (j n) -> p j n", j=PAIRS)[:, :, rest * WIN:P],
                           zerob[:, 0:P - rest * WIN].unsqueeze(1).to_broadcast([P, PAIRS, P - rest * WIN]), saturate=False)
            copy_windows((BLOCKS - 1) * WPB, rest, 0)
            act.wait_ge(s_evac, WSLOTS + WINDOWS)
            act.dma_start(counts_d[(BLOCKS - 1) * P:BLOCKS * P, :], acc[:, 0, :]).then_inc(s_flush[0], 16)

            for k in range(2):
                act.wait_ge(s_flush[k], 16 * (BLOCKS // 2 + (k < BLOCKS % 2) + 1))
            act.wait_ge(s_gfree, GROUPS * (TURNS + 1))
            for g in range(GROUPS):
                act.wait_ge(s_vsp[g], 16 * (TURNS + 1))
            for g0, ng in ((0, VPC), (VPC, 2)):
                for c in range(CHUNKS):
                    last = nc.scalar.copy(seq_r[:, g0 * P:(g0 + ng) * P].rearrange("p (g c h) -> p g c h", c=CHUNKS, h=HEADS)[:, :, c, :],
                                          key[:, VPC - 1 + g0 + c * VPC:VPC - 1 + g0 + ng + c * VPC].unsqueeze(2).to_broadcast([P, ng, HEADS]))
            last.then_inc(s_keyx, 1)

            act.wait_ge(s_sub, 1)
            nc.scalar.activation(seq_s[:, 0:SEQ], seq_s[:, 0:SEQ], ACT.Exp, scale=float(DK) ** -0.5).then_inc(s_exp, 1)
            al = scores[:, :, :].rearrange("p (c g) h -> p g c h", g=VPC)
            for n, (g0, ng) in enumerate(G_BATCHES):
                act.wait_ge(s_alT, n + 1)
                for g in range(g0, g0 + ng):
                    last = nc.scalar.copy(al[:, g, :, :], bank(n % 2)[:, (g - g0) * P:(g - g0 + 1) * P].rearrange("p (c h) -> p c h", h=HEADS))
                last.then_inc(s_alc, 1)
            act.wait_ge(s_sum, GROUPS * (TURNS + 1))
            for k, (a, n) in enumerate(CH):
                nc.scalar.copy(sumT[:, a:a + n], bank(k, n)).then_inc(s_attc, 1)
            def layernorm_root(turn):
                act.wait_ge(s_lnv, turn)
                nc.scalar.activation(hT[:, :], x1[:, :] if turn == 1 else x_again[:, :], ACT.Square).then_inc(s_sq, 1)
                act.wait_ge(s_lnc, turn)
                nc.scalar.activation(ln_var[:, :], ln_sum[:, :], ACT.Sqrt, bias=eps_col[:, :], scale=1.0 / D).then_inc(s_lnr, 1)
            layernorm_root(1)
            for n, (b0, nb) in enumerate(X_BATCHES):
                act.wait_ge(s_ht, n + 1)
                nc.scalar.copy(hT[:, b0 * P:(b0 + nb) * P], bank(n % 2)[:, 0:nb * P]).then_inc(s_htc, 1)
            for k, (a, n) in enumerate(CH):
                act.wait_ge(s_ctt, k + 1)
                nc.scalar.copy(countT[:, a:a + n], bank(2 + k % 2, n)[0:TYPES, :]).then_inc(s_ctc, 1)
            LB = len(X_BATCHES)
            with act.Fori(0, STEPS) as s:
                for n, (b0, nb) in enumerate(X_BATCHES):
                    act.wait_ge(s_hn, s * LB + n + 1)
                    nc.scalar.copy(h_hi[:, b0 * P:(b0 + nb) * P], bank(n % 2, nb * P)).then_inc(s_hh, 1)
                    act.wait_ge(s_hd, s * LB + n + 1)
                    nc.scalar.mul(h_lo[:, b0 * P:(b0 + nb) * P], rT[:, n % 2, 0:nb * P], LO).then_inc(s_hl, 1)

                def chunk(c, blocks):
                    n = blocks * P
                    t = s * ACC_BANKS + c
                    for k in range(blocks):
                        act.wait_ge(s_dense, s * BLOCKS + c * 4 + k + 5)
                        nc.scalar.copy(s_hi[:, k % 2, :], bank(2 * (k % 2))).then_inc(s_shi, 1)
                    act.wait_ge(s_r, t + 1)
                    nc.scalar.copy(rT[:, 0, 0:n], bank(4, n)).then_inc(s_rTc, 1)
                    act.wait_ge(s_g1, t + 1)
                    nc.scalar.activation(gates[:, 0, 0, 0:n], bank(5, n), ACT.Sigmoid, bias=brz[:, 0:1]).then_inc(s_sr, 1)
                    nc.scalar.activation(gates[:, 0, 1, 0:n], bank(6, n), ACT.Sigmoid, bias=brz[:, 1:2]).then_inc(s_sz, 1)
                    act.wait_ge(s_np, t + 1)
                    nc.scalar.activation(gates[:, 0, 2, 0:n], gates[:, 0, 2, 0:n], ACT.Tanh, bias=bih[:, 2:3]).then_inc(s_tn, 1)

                with act.Fori(0, ACC_BANKS - 1) as c:
                    chunk(c, 4)
                chunk(ACC_BANKS - 1, BLOCKS - 4 * (ACC_BANKS - 1))
            act.wait_ge(s_flag, 1)
            with act.If(flag_value(act) > 0):
                for n, (b0, nb) in enumerate(X_BATCHES):
                    act.wait_ge(s_fht, n + 1)
                    nc.scalar.copy(hT[:, b0 * P:(b0 + nb) * P], bank(n % 2)[:, 0:nb * P]).then_inc(s_fhtc, 1)
                for g in range(GROUPS):
                    nc.scalar.copy(stage[:, g, :], pair_i[:, g * GRP:(g + 1) * GRP]).then_inc(s_mstage, 1)
                with act.Fori(0, STEPS) as s:
                    with act.Fori(0, TURNS) as i:
                        for g in range(GROUPS):
                            act.wait_ge(s_mg[g], 16 * GRP * (s * TURNS + i + 1))
                            act.nop(nofuse=True)
                            nc.scalar.copy(stage[:, g, :], pair_i[:, bass.ds(i * TURN + TURN + g * GRP, GRP)]).then_inc(s_mstage, 1)
                    act.wait_ge(s_msum, GROUPS * TURNS * (s + 1) + GROUPS)
                    for k in (0, 2, 4, 6):
                        a, n = CH[k]
                        nc.scalar.copy(sumT[:, a:a + n], bank(k, n)).then_inc(s_sumA, 1)
                    for k, (a, n) in enumerate(CH):
                        p = k % 2
                        act.wait_ge(s_gate, s * len(CH) + k + 1)
                        nc.scalar.activation(gates[:, p, 0, 0:n], bank(4 * p, n), ACT.Sigmoid, bias=brz[:, 0:1])
                        nc.scalar.activation(gates[:, p, 1, 0:n], bank(4 * p + 1, n), ACT.Sigmoid, bias=brz[:, 1:2]).then_inc(s_rz, 1)
                        act.wait_ge(s_npre, s * len(CH) + k + 1)
                        nc.scalar.activation(gates[:, p, 2, 0:n], gates[:, p, 2, 0:n], ACT.Tanh, bias=bih[:, 2:3]).then_inc(s_tanh, 1)
            layernorm_root(2)

        @block.vector
        def _(dve):
            ch = Chain(dve, "dve_chain")
            link = ch.link
            V = nc.vector
            full = (BLOCKS - 1) * P
            V.memset(x_nat[:, full:full + D], 0.0).then_inc(s_xpad, 1)
            V.memset(zerob[:, :], 0.0)
            V.memset(ones[:, :], 1.0)
            V.memset(eps_col[:, :], EPS)
            V.memset(row_carry[:, :], 0.0)
            V.memset(key[:, 0:VPC], -2.0)
            V.memset(key[:, VPC + VISITS:], -3.0)
            V.memset(onesb[:, :], 1.0)
            dve.wait_ge(s_iota, 3)
            V.tensor_copy(wvisit_col[:, :], wtile_i[:, :])
            V.tensor_copy(iota_w, ints)
            V.tensor_copy(iota_row[:, :], ints[:, 0:P])
            link(V.tensor_copy(visit_col[:, :], visit_i[:, :]))
            link(V.tensor_copy(iota_col[:, :], visit_col[:, 0:1]))
            link(V.tensor_scalar(limit[:, :], iota_row[:, 0:BLOCKS - 1], float(P), float(P), ALU.mult, ALU.add))
            link(V.tensor_scalar(limit_w, iota_w[:, 0:WINDOWS], float(WIN), float(WIN), ALU.mult, ALU.add))
            V.tensor_scalar(ident[:, :], iota_row[:, :], iota_col[:, :], None, ALU.is_equal)
            V.tensor_scalar(identb[:, :], iota_row[:, :], iota_col[:, :], None, ALU.is_equal).then_inc(s_const, 1)
            dve.wait_ge(s_last, 16)
            link(V.tensor_copy(last_dstf[:, :], last_dst[:, :]))
            V.tensor_tensor(below[:, :, :], last_dstf[:, :].unsqueeze(2).to_broadcast([P, VROWS, BLOCKS - 1]),
                            limit[:, :].unsqueeze(1).to_broadcast([P, VROWS, BLOCKS - 1]), ALU.is_lt)
            V.tensor_tensor(below_w, last_dstf[:, :].unsqueeze(2).to_broadcast([P, VROWS, WINDOWS]),
                            limit_w.unsqueeze(1).to_broadcast([P, VROWS, WINDOWS]), ALU.is_lt).then_inc(s_below, 1)
            dve.wait_ge(s_left, 1)
            link(V.tensor_tensor(leave[:, :], bank(4)[0:BLOCKS - 1, 0:1], iota_col[0:BLOCKS - 1, :], ALU.add))
            V.tensor_scalar(passed, iota_w[0:BLOCKS - 1, 0:VPAD], leave[:, :], None, ALU.is_gt)
            wlast = WINDOWS - (WK - 1) * P
            V.tensor_tensor(wleave[:, 0:WK - 1], bank(4)[:, 8:8 + WK - 1], visit_col[:, 0:WK - 1], ALU.add)
            link(V.tensor_tensor(wleave[0:wlast, WK - 1:WK], bank(4)[0:wlast, 8 + WK - 1:8 + WK], visit_col[0:wlast, WK - 1:WK], ALU.add))
            for k in range(WK):
                n = P if k < WK - 1 else wlast
                last = V.tensor_scalar(passed_w[0:n, k, :], iota_w[0:n, :], wleave[0:n, k:k + 1], None, ALU.is_gt)
            last.then_inc(s_passed, 1)
            V.tensor_tensor(row_w[0:1, 0:BANK], bank(6)[0:1, :], iota_w[0:1, 0:BANK], ALU.add)
            link(V.tensor_tensor(row_w[0:1, BANK:WINDOWS], bank(7)[0:1, 0:WINDOWS - BANK], iota_w[0:1, BANK:WINDOWS], ALU.add))
            link(V.tensor_scalar(wleave_row[:, :], row_w[0:1, 0:WINDOWS], float(1 + WGRP), None, ALU.add))
            V.memset(flag_f[:, :], 0.0).then_inc(s_wrow, 1)
            dve.wait_ge(s_blk, 1)
            link(V.tensor_scalar(block_first[:, :], bank(5)[:, 0:VROWS], float(P), None, ALU.mult))
            link(V.tensor_tensor(tile_f[:, :], visit_col[:, :], bank(5)[:, 0:VROWS], ALU.subtract))
            V.tensor_copy(tile_i[:, :], tile_f[:, :])
            V.tensor_scalar(window_first[:, :], bank(5)[:, 8:8 + WROWS], float(WIN), None, ALU.mult)
            link(V.tensor_tensor(wtile_f[:, :], wvisit_col[:, :], bank(5)[:, 8:8 + WROWS], ALU.subtract))
            V.tensor_copy(wtile_i[:, :], wtile_f[:, :])

            def pack(row, n, bits, to, extra):
                part = row.rearrange("a (q k) -> a q k", k=4)
                acc_ = row_first[0:1, 0:n // 4]
                link(V.scalar_tensor_tensor(out=acc_, in0=part[:, :, 1], scalar=float(1 << bits), in1=part[:, :, 0], op0=ALU.mult, op1=ALU.add))
                link(V.scalar_tensor_tensor(out=acc_, in0=part[:, :, 2], scalar=float(1 << 2 * bits), in1=acc_, op0=ALU.mult, op1=ALU.add))
                link(V.scalar_tensor_tensor(out=acc_, in0=part[:, :, 3], scalar=float(1 << 3 * bits), in1=acc_, op0=ALU.mult, op1=ALU.add))
                if extra is None:
                    return V.tensor_copy(to, acc_)
                return V.tensor_tensor(to, acc_, extra, ALU.add)

            V.tensor_copy(row_w[0:1, 0:BANK], bank(6)[0:1, :])
            link(V.tensor_copy(row_w[0:1, BANK:VPAD], bank(7)[0:1, 0:VPAD - BANK]))
            link(pack(row_w[0:1, 0:VPAD], VPAD, 5, visit_off[:, :], None))
            quarter = WPAD // 4
            for k in range(4):
                last = V.tensor_copy(row_w[0:1, k * quarter:(k + 1) * quarter], bank(k)[0:1, 0:quarter])
            link(last)
            link(V.tensor_copy(ints[0:1, :], row_w[0:1, :]))
            link(V.tensor_scalar(ints[0:1, :], ints[0:1, :], WSLOTS - 1, None, ALU.bitwise_and))
            link(V.tensor_scalar(limit_w[0:1, 0:WPAD // 4], row_w[0:1, :].rearrange("a (q k) -> a q k", k=4)[:, :, 3], 1.0, 256.0, ALU.add, ALU.mult))
            link(V.tensor_copy(row_w[0:1, :], ints[0:1, :]))
            pack(row_w[0:1, :], WPAD, 2, wrow[:, :], limit_w[0:1, 0:WPAD // 4]).then_inc(s_tile, 1)
            dve.wait_ge(s_we, 16 * WROWS)
            f = [a.rearrange("p (r e) -> p r e", r=WROWS) for a in wf]
            dve.wait_ge(s_tile, 1)
            V.tensor_copy(f[0], wedges[:, :, 1, :])
            link(V.tensor_copy(f[1], wedges[:, :, 0, :]))
            link(V.tensor_scalar(whi_i, wedges[:, :, 0, :], 7, None, ALU.logical_shift_right))
            link(V.tensor_tensor(f[0], f[0], window_first[:, :].unsqueeze(2).to_broadcast([P, WROWS, P]), ALU.subtract))
            V.scalar_tensor_tensor(out=f[1], in0=whi_i, scalar=-float(P), in1=f[1], op0=ALU.mult, op1=ALU.add)
            link(V.scalar_tensor_tensor(out=f[2], in0=whi_i, scalar=float(TYPES), in1=wedges[:, :, 2, :], op0=ALU.mult, op1=ALU.add))
            link(V.scalar_tensor_tensor(out=f[2], in0=f[2], scalar=float(WIN), in1=f[0], op0=ALU.mult, op1=ALU.add))
            link(V.tensor_scalar(f[3], f[0], 0.0, None, ALU.is_ge))
            link(V.scalar_tensor_tensor(out=f[3], in0=f[0], scalar=float(WIN), in1=f[3], op0=ALU.is_lt, op1=ALU.mult))
            link(V.scalar_tensor_tensor(out=f[2], in0=f[2], scalar=1.0, in1=f[3], op0=ALU.add, op1=ALU.mult))
            V.tensor_scalar(f[2], f[2], -1.0, None, ALU.add).then_inc(s_wff, 1)
            dve.wait_ge(s_wft, 2)
            V.tensor_copy(low[:, :], PS[:, 0:WPAD])
            V.tensor_copy(cell[:, :], PS[:, 4 * BANK:4 * BANK + WPAD]).then_inc(s_off, 1)
            dve.wait_ge(s_b, 16 * 8)
            V.tensor_tensor(brz[:, :], bih[:, 0:2], bhh[:, 0:2], ALU.add)
            for b in range(BLOCKS):
                dve.wait_ge(s_qkv, b + 1)
                ps = bank(b % 4, 3 * D)
                V.tensor_tensor(q_nat[:, b * P:(b + 1) * P], ps[:, 0:D], bqkv_b[:, 0:D], ALU.add)
                V.tensor_tensor(kv_st[:, b * 2 * D:(b + 1) * 2 * D], ps[:, D:3 * D], bqkv_b[:, D:3 * D], ALU.add).then_inc(s_qkvc, 1)
            dve.wait_ge(s_ve, 16 * VROWS)
            link(V.tensor_copy(dst_v, visit_edges[:, :, 1, :]))
            V.tensor_copy(src_v, visit_edges[:, :, 0, :])
            V.tensor_copy(key_v, visit_edges[:, :, 2, :])
            link(V.tensor_tensor(rel_v, dst_v, block_first[:, :].unsqueeze(2).to_broadcast([P, VROWS, P]), ALU.subtract))
            link(V.tensor_scalar(ge0_v, rel_v, 0.0, None, ALU.is_ge))
            link(V.scalar_tensor_tensor(out=pair_v, in0=src_v, scalar=float(TYPES), in1=key_v, op0=ALU.mult, op1=ALU.add))
            link(V.scalar_tensor_tensor(out=ge0_v, in0=rel_v, scalar=float(P), in1=ge0_v, op0=ALU.is_lt, op1=ALU.mult))
            V.scalar_tensor_tensor(out=key_v, in0=dst_v, scalar=1.0, in1=ge0_v, op0=ALU.add, op1=ALU.mult).then_inc(s_vf, 1)
            for part, (r0, nr) in enumerate(FIELD_PARTS):
                dve.wait_ge(s_vt, part + 1)
                n = min(nr * P, VISITS - r0 * P)
                V.tensor_copy(rel[:, r0 * P:r0 * P + nr * P], bank(4, nr * P))
                V.tensor_copy(key[:, VPC + r0 * P:VPC + r0 * P + n], bank(5, n))
                V.tensor_copy(src_i[:, r0 * P:r0 * P + nr * P], bank(6, nr * P))
                V.tensor_copy(pair_i[:, r0 * P:r0 * P + nr * P], bank(7, nr * P)).then_inc(s_vfree, 1)
            dve.wait_ge(s_vfree, len(FIELD_PARTS))
            link(V.tensor_copy(pair_i[:, VISITS:VISITS + TURN], pair_i[:, 0:TURN]))
            types_i, types_f = dst_v.rearrange("p r e -> p (r e)").bitcast(i32), rel_v.rearrange("p r e -> p (r e)")
            link(V.tensor_scalar(types_i, pair_i[:, :], TYPES - 1, None, ALU.bitwise_and))
            link(V.tensor_copy(types_f, types_i))
            V.tensor_tensor(types_b[:, :, :], types_f.unsqueeze(2).to_broadcast([P, VPAD, TYPES]),
                            iota_row[:, 0:TYPES].unsqueeze(1).to_broadcast([P, VPAD, TYPES]), ALU.is_equal).then_inc(s_vi, 1)

            def build_onehot(to, v):
                return V.tensor_tensor(to, rel[:, bass.ds(v, GRP)].unsqueeze(2).to_broadcast([P, GRP, P]),
                                       iota_row[:, :].unsqueeze(1).to_broadcast([P, GRP, P]), ALU.is_equal)

            dve.wait_ge(s_kvd, 16 * len(X_BATCHES))
            dve.sem_inc(s_gfree, GROUPS)
            dve.wait_ge(s_vi, 1)
            for k in range((WCOLS + P - 1) // P):
                n = min(P, WCOLS - k * P)
                last = V.tensor_scalar(iota_h[:, k * P:k * P + n], iota_row[:, 0:n], float(k * P), None, ALU.add)
            link(last)
            for g in range(GROUPS):
                V.tensor_copy(stage[:, g, :], src_i[:, g * GRP:(g + 1) * GRP]).then_inc(s_stage, 1)
            lc = Chain(dve, "dve_score_chain")
            with dve.Fori(0, TURNS) as i:
                lc.turn(i, 2 * GROUPS)
                for g in range(GROUPS):
                    build_onehot(onehot_b[:, g, :, :], i * TURN + g * GRP).then_inc(s_oh, 1)
                    v0 = i * (GROUPS * WGRP) + g * WGRP
                    V.tensor_copy(cell_st[:, g % 2, :], cell[:, bass.ds(v0, WGRP)])
                    lc.link(V.tensor_copy(low_st[:, g % 2, :], low[:, bass.ds(v0, WGRP)]))
                    for j in range(WGRP):
                        if j % (WGRP // 2) == 0:
                            dve.wait_ge(s_wvis, v0 + j + WGRP // 2)
                        V.tensor_scalar(cells[:, j, :], iota_h, cell_st[:, g % 2, j:j + 1], None, ALU.is_equal)
                        V.tensor_scalar(lows[:, j, :], iota_row[:, :], low_st[:, g % 2, j:j + 1], None, ALU.is_equal).then_inc(s_wfree, 1)
                        if j == 1:
                            dve.wait_ge(s_oht, i * GROUPS + g + 1)
                            V.tensor_copy(onehotT[:, g, :, :], psT(g).rearrange("p (j e) -> p j e", j=GRP)).then_inc(s_ohtc, 1)
                    dve.wait_ge(s_qe, i * GROUPS + g + 1)
                    dve.wait_ge(s_g[g], 16 * GRP * (i + 1))
                    p = prod[:, g % 2, :]
                    lc.link(V.tensor_tensor(p.rearrange("p (j c) -> p j c", j=GRP), kv_g[:, g, :, 0:D],
                                            bank(6 + g % 2).rearrange("p (j c) -> p j c", j=GRP), ALU.mult))
                    dve.nop(nofuse=True)
                    V.tensor_copy(stage[:, g, :], src_i[:, bass.ds(i * TURN + TURN + g * GRP, GRP)]).then_inc(s_stage, 1)
                    V.tensor_reduce(scores[:, bass.ds(i * TURN + g * GRP, GRP), :],
                                    p.rearrange("p (j h c) -> p j h c", j=GRP, h=HEADS), AX, ALU.add).then_inc(s_gfree, 1)
            dve.wait_ge(s_qe, GROUPS * TURNS)
            V.tensor_copy(count_sb[:, :], PS[:, COUNT_OFF:COUNT_OFF + PAIRS]).then_inc(s_cnt, 1)

            for g in range(GROUPS):
                dve.wait_ge(s_vsp[g], 16 * (TURNS + 1))
            for k in range(2):
                dve.wait_ge(s_flush[k], 16 * (BLOCKS // 2 + (k < BLOCKS % 2) + 1))
            dve.wait_ge(s_gfree, GROUPS * (TURNS + 1))
            V.tensor_copy(seq_b[:, 0:SEQ].rearrange("p (g c h) -> p g c h", c=CHUNKS, h=HEADS),
                          scores[:, :, :].rearrange("p (c g) h -> p g c h", g=VPC)).then_inc(s_scx, 1)
            for n in range(len(G_BATCHES) + 1):
                dve.wait_ge(s_keyT, n + 1)
                if n < len(G_BATCHES):
                    g0, ng = G_BATCHES[n]
                    V.tensor_copy(seq_a[:, 1 + g0 * P:1 + (g0 + ng) * P], bank(n % 2, ng * P)).then_inc(s_keyTc, 1)
                else:
                    V.tensor_copy(seq_a[:, 0:1], bank(n % 2)[:, 0:1])
                    link(V.tensor_copy(seq_a[:, SEQ + 1:SEQ + 2], bank(n % 2)[:, 1:2]))
            link(V.tensor_tensor(seq_r[:, 0:SEQ + 1], seq_a[:, 1:SEQ + 2], seq_a[:, 0:SEQ + 1], ALU.not_equal))
            link(V.tensor_scalar(seq_r[:, 0:SEQ + 1], seq_r[:, 0:SEQ + 1], -BIG, None, ALU.mult))
            for n, (g0, ng) in enumerate(G_BATCHES):
                dve.wait_ge(s_scT, n + 1)
                ins = V.tensor_copy(seq_s[:, g0 * P:(g0 + ng) * P], bank(2 + n % 2, ng * P))
                ins.then_inc(s_scTc, 1)
            dve.wait_ge(s_scTc, len(G_BATCHES))

            scans = [0]

            def scan(data, to, reverse, op0, op1, initial):
                reset = seq_r[:, 1:SEQ + 1] if reverse else seq_r[:, 0:SEQ]
                data, to = data[:, 0:SEQ], to[:, 0:SEQ]
                if reverse:
                    data, to, reset = data[:, ::-1], to[:, ::-1], reset[:, ::-1]
                link(V.tensor_tensor_scan(to, reset, data, initial, op0, op1))

            def full_scan(data, to, scratch, reverse, op0, op1, start):
                scan(data, scratch, reverse, op0, op1, start)
                end = 0 if reverse else SEQ - 1
                V.tensor_copy(col_last[:, :], scratch[:, end:end + 1])
                span = seq_r[:, 1:SEQ + 1] if reverse else seq_r[:, 0:SEQ]
                V.tensor_reduce(col_pass[:, :], span, AX, ALU.min).then_inc(s_cols, 1)
                scans[0] += 1
                n = scans[0]
                dve.wait_ge(s_cr, n)
                swap = "a (c h) -> a h c"
                V.tensor_copy(row_last[:, :].rearrange("a (h c) -> a h c", h=HEADS), bank(4)[0:1, 0:P].rearrange(swap, h=HEADS))
                link(V.tensor_copy(row_pass[:, :].rearrange("a (h c) -> a h c", h=HEADS), bank(5)[0:1, 0:P].rearrange(swap, h=HEADS)))
                rows = [row_end[:, :], row_pass[:, :], row_last[:, :]]
                if reverse:
                    rows = [r[:, ::-1] for r in rows]
                link(V.tensor_tensor_scan(rows[0], rows[1], rows[2], start, op0, op1))
                ends = row_end[:, :].rearrange("a (h c) -> a c h", h=HEADS)
                carry = row_carry[:, :].rearrange("a (c h) -> a c h", h=HEADS)
                if reverse:
                    V.tensor_copy(carry[:, 0:CHUNKS - 1, :], ends[:, 1:CHUNKS, :]).then_inc(s_crc, 1)
                else:
                    V.tensor_copy(carry[:, 1:CHUNKS, :], ends[:, 0:CHUNKS - 1, :]).then_inc(s_crc, 1)
                dve.wait_ge(s_cc, n)
                link(V.tensor_copy(col_carry[:, :], bank(6)[:, 0:1]))
                scan(data, to, reverse, op0, op1, col_carry[:, :])

            full_scan(seq_s, seq_a, seq_b, False, ALU.add, ALU.max, -BIG)
            full_scan(seq_a, seq_b, seq_b, True, ALU.add, ALU.max, -BIG)
            V.tensor_tensor(seq_s[:, 0:SEQ], seq_s[:, 0:SEQ], seq_b[:, 0:SEQ], ALU.subtract).then_inc(s_sub, 1)
            link(V.tensor_scalar(seq_r[:, 0:SEQ + 1], seq_r[:, 0:SEQ + 1], 0.0, None, ALU.is_equal))
            link(V.memset(row_carry[:, :], 0.0))
            dve.wait_ge(s_exp, 1)
            full_scan(seq_s, seq_a, seq_b, False, ALU.mult, ALU.add, 0.0)
            full_scan(seq_a, seq_b, seq_b, True, ALU.mult, ALU.max, 0.0)
            link(V.reciprocal(seq_a[:, 0:SEQ], seq_b[:, 0:SEQ]))
            V.tensor_tensor(seq_s[:, 0:SEQ], seq_s[:, 0:SEQ], seq_a[:, 0:SEQ], ALU.mult).then_inc(s_alpha, 1)

            dve.wait_ge(s_alT, len(G_BATCHES))
            V.memset(x_again[:, full:full + D], 0.0).then_inc(s_xpad, 1)
            dve.wait_ge(s_alc, len(G_BATCHES))
            dve.sem_inc(s_av, GROUPS)
            with dve.Fori(0, TURNS) as i:
                for g in range(GROUPS):
                    dve.wait_ge(s_sum, i * GROUPS + g + 1)
                    dve.nop(nofuse=True)
                    build_onehot(onehot[:, g, :, :], i * TURN + g * GRP)
                    dve.wait_ge(s_vin[g], 16 * (i + 1))
                    dve.nop(nofuse=True)
                    V.tensor_tensor(av[:, g, :, :].rearrange("p j (h c) -> p j h c", h=HEADS),
                                    g_ring[:, g, :, :].rearrange("p j (h c) -> p j h c", h=HEADS),
                                    scores[:, bass.ds(i * TURN + g * GRP, GRP), :].unsqueeze(3).to_broadcast([P, GRP, HEADS, DK]),
                                    ALU.mult).then_inc(s_av, 1)
            dve.wait_ge(s_x2, 32)
            link(V.tensor_tensor(x_again.rearrange("p (b c) -> p b c", c=D), x_again.rearrange("p (b c) -> p b c", c=D),
                                 bo_b[:, :].unsqueeze(1).to_broadcast([P, BLOCKS, D]), ALU.add))
            for n, (b0, nb) in enumerate(X_BATCHES):
                dve.wait_ge(s_o, n + 1)
                link(V.tensor_tensor(x_again[:, b0 * P:(b0 + nb) * P], x_again[:, b0 * P:(b0 + nb) * P], bank(n, nb * P), ALU.add))

            def layernorm(frm, centred, to, turn):
                def nodes(a):
                    return a.rearrange("p (b c) -> p b c", c=D)
                link(V.tensor_reduce(ln_sum[:, :], nodes(frm), AX, ALU.add))
                link(V.tensor_scalar(ln_sum[:, :], ln_sum[:, :], 1.0 / D, None, ALU.mult))
                V.tensor_tensor(nodes(centred), nodes(frm), ln_sum[:, :].unsqueeze(2).to_broadcast([P, BLOCKS, D]),
                                ALU.subtract).then_inc(s_lnv, 1)
                dve.wait_ge(s_sq, turn)
                V.tensor_reduce(ln_sum[:, :], nodes(hT), AX, ALU.add).then_inc(s_lnc, 1)
                dve.wait_ge(s_lnr, turn)
                link(V.reciprocal(ln_sum[:, :], ln_var[:, :]))
                return V.tensor_tensor(nodes(to), nodes(centred), ln_sum[:, :].unsqueeze(2).to_broadcast([P, BLOCKS, D]), ALU.mult)

            dve.sem_inc(s_chk, 1)
            layernorm(x_again, x1, x1, 1).then_inc(s_x1, 1)

            dc = Chain(dve, "dve_dense_chain")
            LB = len(X_BATCHES)
            with dve.Fori(0, STEPS) as s:
                for n, (b0, nb) in enumerate(X_BATCHES):
                    dve.wait_ge(s_hh, s * LB + n + 1)
                    V.tensor_tensor(rT[:, n % 2, 0:nb * P], bank(n % 2, nb * P), h_hi[:, b0 * P:(b0 + nb) * P], ALU.subtract).then_inc(s_hd, 1)

                def chunk(c, blocks, k_check):
                    n = blocks * P
                    t = s * ACC_BANKS + c
                    dc.turn(t, 3)
                    for k in range(blocks):
                        dve.wait_ge(s_cin[k], 16 * (s * (ACC_BANKS - (k >= BLOCKS % 4)) + c + 1))
                    dve.nop(nofuse=True)
                    V.tensor_reduce(codes[:, bass.ds(t, 1)], ringu[:, bass.ds(k_check * (4 * BLK_I), 4 * BLK_I)], AX, ALU.max).then_inc(s_chk, 1)
                    for k in range(blocks):
                        b = s * BLOCKS + c * 4 + k
                        dve.wait_ge(s_shi, b + 1)
                        dve.nop(nofuse=True)
                        V.scalar_tensor_tensor(out=sum_b[:, k, :], in0=bank(2 * (k % 2) + 1), scalar=1.0 / LO, in1=s_hi[:, k % 2, :],
                                               op0=ALU.mult, op1=ALU.add).then_inc(s_sb, 1)
                    r, z, q, h = gates[:, 0, 0, 0:n], gates[:, 0, 1, 0:n], gates[:, 0, 2, 0:n], hT[:, bass.ds(c * BANK, n)]
                    dve.wait_ge(s_sr, t + 1)
                    dc.link(V.scalar_tensor_tensor(out=q, in0=bank(7, n), scalar=bhh[:, 2:3], in1=r, op0=ALU.add, op1=ALU.mult))
                    dve.wait_ge(s_g2, t + 1)
                    V.tensor_tensor(q, q, bank(5, n), ALU.add).then_inc(s_np, 1)
                    dve.wait_ge(s_tn, t + 1)
                    dve.nop(nofuse=True)
                    dc.link(V.tensor_tensor(h, h, q, ALU.subtract))
                    dc.link(V.tensor_tensor(h, h, z, ALU.mult))
                    V.tensor_tensor(h, h, q, ALU.add).then_inc(s_hu, 1)

                with dve.Fori(0, ACC_BANKS - 1) as c:
                    chunk(c, 4, s)
                chunk(ACC_BANKS - 1, BLOCKS - 4 * (ACC_BANKS - 1), 0)
            dve.wait_ge(s_chk, STEPS * ACC_BANKS + 1)
            V.tensor_reduce(code_max[:, :], codes[:, :], AX, ALU.max).then_inc(s_cm, 1)
            dve.wait_ge(s_cmr, 1)
            link(V.tensor_reduce(flag_f[:, :], bank(0)[0:1, 0:P], AX, ALU.max))
            V.tensor_scalar(flag_i[:, :], flag_f[:, :], float(EXACT_CODE), None, ALU.is_ge).then_inc(s_flag, 1)
            dve.wait_ge(s_flag, 1)
            with dve.If(flag_value(dve) > 0):
                gc = Chain(dve, "dve_gru_chain")
                for k in range(4):
                    dve.sem_inc(s_md[k], 16)
                with dve.Fori(0, STEPS) as s:
                    for b in range(BLOCKS):
                        dve.wait_ge(s_m, s * BLOCKS + b + 1)
                        dve.wait_ge(s_md[b % 4], 16 * (s * len(range(b % 4, BLOCKS, 4)) + b // 4 + 1))
                        V.tensor_tensor(msg_st[:, b % 4, :], bank(b % 4), bmsg_b[:, :], ALU.add).then_inc(s_mc, 1)
                    with dve.Fori(0, TURNS) as i:
                        for g in range(GROUPS):
                            dve.wait_ge(s_msum, (s * TURNS + i) * GROUPS + g + 1)
                            dve.nop(nofuse=True)
                            build_onehot(onehot[:, g, :, :], i * TURN + g * GRP).then_inc(s_moh, 1)
                    dve.wait_ge(s_msum, GROUPS * TURNS * (s + 1) + GROUPS)
                    for k in (1, 3, 5):
                        a, n = CH[k]
                        V.tensor_copy(sumT[:, a:a + n], bank(k, n)).then_inc(s_sumV, 1)
                    gc.turn(s, 3 * len(CH))
                    for k, (a, n) in enumerate(CH):
                        p = k % 2
                        r, z, t, h = gates[:, p, 0, 0:n], gates[:, p, 1, 0:n], gates[:, p, 2, 0:n], hT[:, a:a + n]
                        dve.wait_ge(s_rz, s * len(CH) + k + 1)
                        gc.link(V.scalar_tensor_tensor(out=t, in0=bank(4 * p + 3, n), scalar=bhh[:, 2:3], in1=r, op0=ALU.add, op1=ALU.mult))
                        V.tensor_tensor(t, t, bank(4 * p + 2, n), ALU.add).then_inc(s_npre, 1)
                        dve.wait_ge(s_tanh, s * len(CH) + k + 1)
                        gc.link(V.tensor_tensor(h, h, t, ALU.subtract))
                        gc.link(V.tensor_tensor(h, h, z, ALU.mult))
                        V.tensor_tensor(h, h, t, ALU.add).then_inc(s_h, 1)
            for n, (b0, nb) in enumerate(X_BATCHES):
                dve.wait_ge(s_fin, n + 1)
                link(V.tensor_tensor(x1[:, b0 * P:(b0 + nb) * P], x1[:, b0 * P:(b0 + nb) * P], bank(1 + n, nb * P), ALU.add))
            layernorm(x1, x_again, x_again, 2).then_inc(s_y, 1)

        @block.tensor
        def _(pe):
            T = nc.tensor

            def tr(to, frm, k=P, idn=None):
                return T.transpose(to, frm, (ident if idn is None else idn)[0:k, 0:k])

            pe.wait_ge(s_const, 1)
            pe.wait_ge(s_w, 16 * NW)
            for n, (k0, nk) in enumerate(W_BATCHES):
                if n >= 2:
                    pe.wait_ge(s_wc, n - 1)
                for k in range(k0, k0 + nk):
                    last = tr(bank(n % 2)[:, (k - k0) * D:(k - k0 + 1) * D], w_nat[:, k, :])
                last.then_inc(s_wt, 1)
            pe.wait_ge(s_x, 32)
            for n, (b0, nb) in enumerate(X_BATCHES):
                if n >= 2:
                    pe.wait_ge(s_xc, n - 1)
                for b in range(b0, b0 + nb):
                    last = tr(bank(2 + n % 2)[:, (b - b0) * P:(b - b0 + 1) * P], x_nat[:, b * P:(b + 1) * P])
                last.then_inc(s_xt, 1)
            pe.wait_ge(s_below, 1)
            for r in range(VROWS):
                T.matmul(bank(4)[0:BLOCKS - 1, 0:1], lhsT=below[:, r, :], rhs=ones[:, 0:1], start=(r == 0), stop=(r == VROWS - 1))
            for k in range(WK):
                n = min(P, WINDOWS - k * P)
                for r in range(VROWS):
                    T.matmul(bank(4)[0:n, 8 + k:9 + k], lhsT=below_w[:, r, k * P:k * P + n], rhs=onesb[:, :], start=(r == 0), stop=(r == VROWS - 1))
            for r in range(VROWS):
                T.matmul(bank(6)[0:1, :], lhsT=onesb[:, :], rhs=below_w[:, r, 0:BANK], start=(r == 0), stop=(r == VROWS - 1))
            for r in range(VROWS):
                last = T.matmul(bank(7)[0:1, 0:WINDOWS - BANK], lhsT=onesb[:, :], rhs=below_w[:, r, BANK:WINDOWS], start=(r == 0), stop=(r == VROWS - 1))
            last.then_inc(s_left, 1)
            pe.wait_ge(s_passed, 1)
            pe.wait_ge(s_wrow, 1)
            pe.wait_ge(s_wc, len(W_BATCHES))
            pe.wait_ge(s_xc, len(X_BATCHES))
            wlast = WINDOWS - (WK - 1) * P
            for r in range(VROWS):
                T.matmul(bank(5)[:, r:r + 1], lhsT=passed[:, r * P:(r + 1) * P], rhs=ones[0:BLOCKS - 1, 0:1], start=True, stop=True)
            for r in range(WROWS):
                for k in range(WK):
                    n = P if k < WK - 1 else wlast
                    T.matmul(bank(5)[:, 8 + r:9 + r], lhsT=passed_w[0:n, k, r * P:(r + 1) * P], rhs=onesb[0:n, :], start=(k == 0), stop=(k == WK - 1))
            quarter = WPAD // 4
            for q in range(4):
                for k in range(WK):
                    n = P if k < WK - 1 else wlast
                    T.matmul(bank(q)[0:1, 0:quarter], lhsT=onesb[0:n, :], rhs=passed_w[0:n, k, q * quarter:(q + 1) * quarter], start=(k == 0), stop=(k == WK - 1))
            T.matmul(bank(6)[0:1, :], lhsT=ones[0:BLOCKS - 1, 0:1], rhs=passed[:, 0:BANK], start=True, stop=True)
            T.matmul(bank(7)[0:1, 0:VPAD - BANK], lhsT=ones[0:BLOCKS - 1, 0:1], rhs=passed[:, BANK:VPAD], start=True, stop=True).then_inc(s_blk, 1)
            pe.wait_ge(s_wff, 1)
            for k in (1, 2):
                for r in range(WROWS):
                    last = tr(PS[:, (k - 1) * 4 * BANK + r * P:(k - 1) * 4 * BANK + (r + 1) * P], wf[k][:, r * P:(r + 1) * P])
                last.then_inc(s_wft, 1)
            pe.wait_ge(s_off, 1)
            pe.wait_ge(s_wc, len(W_BATCHES))
            pe.wait_ge(s_xc, len(X_BATCHES))
            for b in range(BLOCKS):
                if b >= 4:
                    pe.wait_ge(s_qkvc, b - 3)
                T.matmul(bank(b % 4, 3 * D), lhsT=xT[:, b * P:(b + 1) * P], rhs=wqkvT[:, :], start=True, stop=True).then_inc(s_qkv, 1)
            pe.wait_ge(s_vf, 1)
            for part, (r0, nr) in enumerate(FIELD_PARTS):
                if part:
                    pe.wait_ge(s_vfree, part)
                for k, field in enumerate((rel_v, key_v, src_v, pair_v)):
                    for r in range(r0, r0 + nr):
                        last = tr(bank(4 + k)[:, (r - r0) * P:(r - r0 + 1) * P], field[:, r, :])
                last.then_inc(s_vt, 1)

            def load(row, at):
                _, vals = nc.values_load_multi_w_load_instructions(
                    row[0:1, bass.ds(at, 1)], engines=(mybir.EngineType.PE,), min_val=0, max_val=1 << 20)
                return vals[0]

            def block_of(word, j):
                return (word >> (5 * j)) & 31

            def node_of(word, j):
                return nc.s_assert_within(block_of(word, j) * P, 0, PADN - P, skip_runtime_bounds_check_because="the staircase ends at the last block")

            pe.wait_ge(s_qkvc, BLOCKS)
            pe.wait_ge(s_vi, 1)
            T.matmul(PS[:, COUNT_OFF:COUNT_OFF + PAIRS], lhsT=zerob[:, 0:P], rhs=zerob[:, 0:PAIRS], start=True, stop=True)
            for k in range(WSLOTS):
                last = T.matmul(bank(k, WCOLS), lhsT=zerob[:, 0:P], rhs=zerob[:, 0:WCOLS], start=True, stop=True)
            last.then_inc(s_ctz, 1)
            pe.sem_inc(s_wvis, WGRP)
            with pe.Fori(0, TURNS) as i:
                for g in range(GROUPS):
                    word = load(visit_off, i * GROUPS + g)
                    pe.wait_ge(s_oh, i * GROUPS + g + 1)
                    for j in range(GRP):
                        last = tr(psT(g)[:, j * P:(j + 1) * P], onehot_b[:, g, j, :], idn=identb)
                    last.then_inc(s_oht, 1)
                    for j in range(GRP):
                        T.matmul(PS[:, bass.ds(block_of(word, j) * TYPES + COUNT_OFF, TYPES)], lhsT=onehot_b[:, g, j, :],
                                 rhs=types_b[:, bass.ds(i * TURN + g * GRP + j, 1), :].rearrange("p v t -> p (v t)"),
                                 start=False, stop=True, skip_group_check=True)
                    for half in range(2):
                        at = (i * GROUPS + g) * 2 + half
                        where = load(wrow, at)
                        pe.wait_ge(s_wfree, (at + 1) * (WGRP // 2))
                        pe.wait_ge(s_evac, where >> 8)
                        pe.nop(nofuse=True)
                        for jj in range(WGRP // 2):
                            j = half * WGRP // 2 + jj
                            last = T.matmul(PS[:, bass.ds(((where >> (2 * jj)) & 3) * BANK, WCOLS)], lhsT=lows[:, j, :], rhs=cells[:, j, :],
                                            start=False, stop=True, skip_group_check=True)
                            last.then_inc(s_wvis, 1)
                    pe.wait_ge(s_ohtc, i * GROUPS + g + 1)
                    pe.wait_ge(s_gfree, i * GROUPS + g + GROUPS - 1)
                    for j in range(GRP):
                        last = T.matmul(bank(6 + g % 2)[:, j * P:(j + 1) * P], lhsT=onehotT[:, g, j, :],
                                        rhs=q_nat[:, bass.ds(node_of(word, j), P)], start=True, stop=True)
                    last.then_inc(s_qe, 1)

            pe.wait_ge(s_keyx, 1)
            for n in range(len(G_BATCHES) + 1):
                if n >= 2:
                    pe.wait_ge(s_keyTc, n - 1)
                if n < len(G_BATCHES):
                    g0, ng = G_BATCHES[n]
                    for g in range(g0, g0 + ng):
                        last = tr(bank(n % 2)[:, (g - g0) * P:(g - g0 + 1) * P], seq_r[:, (g + 1) * P:(g + 2) * P])
                else:
                    T.matmul(bank(n % 2)[:, 0:1], lhsT=seq_r[:, 0:P], rhs=ident[:, P - 1:P], start=True, stop=True)
                    last = T.matmul(bank(n % 2)[:, 1:2], lhsT=seq_r[:, (VPC + 1) * P:(VPC + 2) * P], rhs=ident[:, 0:1], start=True, stop=True)
                last.then_inc(s_keyT, 1)
            pe.wait_ge(s_scx, 1)
            for n, (g0, ng) in enumerate(G_BATCHES):
                if n >= 2:
                    pe.wait_ge(s_scTc, n - 1)
                for g in range(g0, g0 + ng):
                    last = tr(bank(2 + n % 2)[:, (g - g0) * P:(g - g0 + 1) * P], seq_b[:, g * P:(g + 1) * P])
                last.then_inc(s_scT, 1)
            for n in range(1, 5):
                pe.wait_ge(s_cols, n)
                tr(bank(4)[0:1, 0:P], col_last[:, :])
                tr(bank(5)[0:1, 0:P], col_pass[:, :]).then_inc(s_cr, 1)
                pe.wait_ge(s_crc, n)
                tr(bank(6)[:, 0:1], row_carry[:, :], k=1).then_inc(s_cc, 1)
            pe.wait_ge(s_alpha, 1)
            for n, (g0, ng) in enumerate(G_BATCHES):
                if n >= 2:
                    pe.wait_ge(s_alc, n - 1)
                for g in range(g0, g0 + ng):
                    last = tr(bank(n % 2)[:, (g - g0) * P:(g - g0 + 1) * P], seq_s[:, g * P:(g + 1) * P])
                last.then_inc(s_alT, 1)

            def zero_sums():
                for k, (a, n) in enumerate(CH):
                    T.matmul(bank(k, n), lhsT=zerob[:, 0:P], rhs=zerob[:, 0:n], start=True, stop=True)

            pe.wait_ge(s_alc, len(G_BATCHES))
            zero_sums()
            pe.sem_inc(s_sum, GROUPS)
            with pe.Fori(0, TURNS) as i:
                for g in range(GROUPS):
                    word = load(visit_off, i * GROUPS + g)
                    pe.wait_ge(s_av, i * GROUPS + GROUPS + g + 1)
                    for j in range(GRP):
                        last = T.matmul(PS[:, bass.ds(node_of(word, j), P)], lhsT=av[:, g, j, :], rhs=onehot[:, g, j, :],
                                        start=False, stop=True, skip_group_check=True)
                    last.then_inc(s_sum, 1)
            pe.wait_ge(s_attc, len(CH))
            for n, (b0, nb) in enumerate(X_BATCHES):
                for b in range(b0, b0 + nb):
                    last = T.matmul(bank(n)[:, (b - b0) * D:(b - b0 + 1) * D], lhsT=sumT[:, b * P:(b + 1) * P], rhs=woT[:, :], start=True, stop=True)
                last.then_inc(s_o, 1)
            pe.wait_ge(s_x1, 1)
            for n, (b0, nb) in enumerate(X_BATCHES):
                if n >= 2:
                    pe.wait_ge(s_htc, n - 1)
                for b in range(b0, b0 + nb):
                    last = tr(bank(n % 2)[:, (b - b0) * P:(b - b0 + 1) * P], x1[:, b * P:(b + 1) * P])
                last.then_inc(s_ht, 1)
            for k, (a, n) in enumerate(CH):
                if k >= 2:
                    pe.wait_ge(s_ctc, k - 1)
                for b in range(a // P, (a + n) // P):
                    last = tr(bank(2 + k % 2)[0:TYPES, (b * P - a):(b * P - a) + P], count_sb[:, b * TYPES:(b + 1) * TYPES])
                last.then_inc(s_ctt, 1)
            pe.wait_ge(s_ctc, len(CH))
            pe.wait_ge(s_htc, len(X_BATCHES))
            pe.sem_inc(s_dense, 4)
            pe.sem_inc(s_hu, 1)
            LB = len(X_BATCHES)
            with pe.Fori(0, STEPS) as s:
                pe.wait_ge(s_hu, ACC_BANKS * s + 1)
                for n, (b0, nb) in enumerate(X_BATCHES):
                    if n >= 2:
                        pe.wait_ge(s_hd, s * LB + n - 1)
                    for b in range(b0, b0 + nb):
                        last = tr(bank(n % 2)[:, (b - b0) * P:(b - b0 + 1) * P], hT[:, b * P:(b + 1) * P])
                    last.then_inc(s_hn, 1)
                pe.wait_ge(s_hl, (s + 1) * LB)
                pe.wait_ge(s_hd, (s + 1) * LB)
                pe.nop(nofuse=True)

                def chunk(c, blocks):
                    n = blocks * P
                    t = s * ACC_BANKS + c

                    def messages(k):
                        pe.wait_ge(s_sb, s * BLOCKS + c * 4 + k + 1)
                        for ty in range(TYPES):
                            T.matmul(bank(4)[:, k * P:(k + 1) * P], lhsT=wmsgT[:, ty * D:(ty + 1) * D], rhs=sum_b[:, k, ty * P:(ty + 1) * P],
                                     start=(ty == 0), stop=False)
                        pe.nop(nofuse=True)
                        return T.matmul(bank(4)[:, k * P:(k + 1) * P], lhsT=bmsg_t[:, :], rhs=countT[:, bass.ds(c * BANK + k * P, P)],
                                        start=False, stop=True)

                    for k in range(blocks):
                        pe.wait_ge(s_cin[k], 16 * (s * (ACC_BANKS - (k >= BLOCKS % 4)) + c + 1))
                        pe.nop(nofuse=True)
                        for m in range(BLOCKS):
                            for half, h in ((0, h_hi), (1, h_lo)):
                                last = T.matmul(bank(2 * (k % 2) + half), lhsT=h[:, m * P:(m + 1) * P], rhs=ring8[:, k, m, :],
                                                start=(m == 0), stop=(m == BLOCKS - 1))
                        last.then_inc(s_dense, 1)
                        if k:
                            messages(k - 1)
                    messages(blocks - 1).then_inc(s_r, 1)
                    pe.wait_ge(s_hu, t + 1)
                    h = hT[:, bass.ds(c * BANK, n)]
                    pe.nop(nofuse=True)
                    T.matmul(bank(5, n), lhsT=whhT[:, 0:D], rhs=h, start=True, stop=False)
                    T.matmul(bank(6, n), lhsT=whhT[:, D:2 * D], rhs=h, start=True, stop=False)
                    T.matmul(bank(7, n), lhsT=whhT[:, 2 * D:3 * D], rhs=h, start=True, stop=True)
                    pe.wait_ge(s_rTc, t + 1)
                    m = rT[:, 0, 0:n]
                    T.matmul(bank(5, n), lhsT=wihT[:, 0:D], rhs=m, start=False, stop=True)
                    T.matmul(bank(6, n), lhsT=wihT[:, D:2 * D], rhs=m, start=False, stop=True).then_inc(s_g1, 1)
                    pe.wait_ge(s_sr, t + 1)
                    T.matmul(bank(5, n), lhsT=wihT[:, 2 * D:3 * D], rhs=m, start=True, stop=True).then_inc(s_g2, 1)

                with pe.Fori(0, ACC_BANKS - 1) as c:
                    chunk(c, 4)
                chunk(ACC_BANKS - 1, BLOCKS - 4 * (ACC_BANKS - 1))
            pe.wait_ge(s_hu, ACC_BANKS * STEPS + 1)
            pe.wait_ge(s_cm, 1)
            tr(bank(0)[0:1, 0:P], code_max[:, :]).then_inc(s_cmr, 1)
            pe.wait_ge(s_flag, 1)
            with pe.If(flag_value(pe) > 0):
                for n, (b0, nb) in enumerate(X_BATCHES):
                    if n >= 2:
                        pe.wait_ge(s_fhtc, n - 1)
                    for b in range(b0, b0 + nb):
                        last = tr(bank(n % 2)[:, (b - b0) * P:(b - b0 + 1) * P], x1[:, b * P:(b + 1) * P])
                    last.then_inc(s_fht, 1)
                pe.wait_ge(s_fhtc, len(X_BATCHES))
                pe.sem_inc(s_msum, GROUPS)
                pe.sem_inc(s_h, len(CH))
                with pe.Fori(0, STEPS) as s:
                    pe.wait_ge(s_h, len(CH) * (s + 1))
                    for b in range(BLOCKS):
                        if b >= 4:
                            pe.wait_ge(s_mc, s * BLOCKS + b - 3)
                        T.matmul(bank(b % 4), lhsT=hT[:, b * P:(b + 1) * P], rhs=wmsgT[:, :], start=True, stop=True).then_inc(s_m, 1)
                    pe.wait_ge(s_mc, (s + 1) * BLOCKS)
                    zero_sums()
                    with pe.Fori(0, TURNS) as i:
                        for g in range(GROUPS):
                            word = load(visit_off, i * GROUPS + g)
                            pe.wait_ge(s_moh, (s * TURNS + i) * GROUPS + g + 1)
                            pe.wait_ge(s_mg[g], 16 * GRP * (s * TURNS + i + 1))
                            for j in range(GRP):
                                last = T.matmul(PS[:, bass.ds(node_of(word, j), P)], lhsT=g_ring[:, g, j, :], rhs=onehot[:, g, j, :],
                                                start=False, stop=True, skip_group_check=True)
                            last.then_inc(s_msum, 1)
                    pe.wait_ge(s_sumA, 4 * (s + 1))
                    pe.wait_ge(s_sumV, 3 * (s + 1))
                    for k, (a, n) in enumerate(CH):
                        p = 4 * (k % 2)
                        if k >= 2:
                            pe.wait_ge(s_h, len(CH) * (s + 1) + k - 1)
                        m, h = sumT[:, a:a + n], hT[:, a:a + n]
                        T.matmul(bank(p, n), lhsT=wihT[:, 0:D], rhs=m, start=True, stop=False)
                        T.matmul(bank(p, n), lhsT=whhT[:, 0:D], rhs=h, start=False, stop=True)
                        T.matmul(bank(p + 1, n), lhsT=wihT[:, D:2 * D], rhs=m, start=True, stop=False)
                        T.matmul(bank(p + 1, n), lhsT=whhT[:, D:2 * D], rhs=h, start=False, stop=True)
                        T.matmul(bank(p + 2, n), lhsT=wihT[:, 2 * D:3 * D], rhs=m, start=True, stop=True)
                        T.matmul(bank(p + 3, n), lhsT=whhT[:, 2 * D:3 * D], rhs=h, start=True, stop=True).then_inc(s_gate, 1)

                pe.wait_ge(s_h, len(CH) * (STEPS + 1))
            for n, (b0, nb) in enumerate(X_BATCHES):
                for b in range(b0, b0 + nb):
                    last = tr(bank(1 + n)[:, (b - b0) * P:(b - b0 + 1) * P], hT[:, b * P:(b + 1) * P])
                last.then_inc(s_fin, 1)


_INS = ['x', 'src', 'dst', 'edge_type_4', 'L0_gnn_Wq', 'L0_gnn_bq', 'L0_gnn_Wk', 'L0_gnn_bk', 'L0_gnn_Wv', 'L0_gnn_bv',
        'L0_gnn_Wo', 'L0_gnn_bo', 'L1_gnn_W_msg', 'L1_gnn_b_msg', 'L1_gnn_w_ih', 'L1_gnn_w_hh', 'L1_gnn_b_ih', 'L1_gnn_b_hh']


def kernel(**inputs):
    import numpy as _np
    import concourse.bacc as _bacc
    from concourse import mybir as _mybir
    from concourse.bass_utils import run_bass_kernel_spmd as _run

    nc = _bacc.Bacc("TRN2", target_bir_lowering=False, num_devices=1)
    arrays, args = {}, []
    for name in _INS:
        a = _np.ascontiguousarray(inputs[name])
        arrays[f"in_{name}"] = a
        args.append(nc.dram_tensor(f"in_{name}", a.shape, _mybir.dt.from_np(a.dtype), kind="ExternalInput").ap())
    shape = inputs['x'].shape
    args.append(nc.dram_tensor("out_0", shape, _mybir.dt.float32, kind="ExternalOutput").ap())
    gnn_program(nc, *args)
    r = _run(nc, [arrays], core_ids=[0])
    return r.results[0]["out_0"]
```
